# Optimizing a Trainium2 kernel written in Bass

```python
import numpy as np
import jax
import jax.numpy as jnp

def _softmax(x, axis=-1):
    return jax.nn.softmax(x, axis=axis)

def _gelu(x):
    return jax.nn.gelu(x, approximate=True)

def _silu(x):
    return jax.nn.silu(x)

def _sigmoid(x):
    return jax.nn.sigmoid(x)

def _layernorm(x, axis=-1, eps=1e-05):
    m = jnp.mean(x, axis=axis, keepdims=True)
    v = jnp.var(x, axis=axis, keepdims=True)
    return (x - m) / jnp.sqrt(v + eps)

def _scatter_add(tgt, idx, src, axis=0):
    return tgt.at[idx].add(src)

def _segment_sum(src, seg, n):
    return jax.ops.segment_sum(src, seg, n)
kernel_name = 'mk_perceiver_d1_seqx_r4_97f606'

def setup_inputs(seed: int=0):
    np.random.seed(seed)
    _w = jnp.asarray

    def _rec_inputs():
        import jax
        import jax.numpy as jnp
        _rk = jax.random.key(seed)
        x = -0.0002928 + 1 * jax.random.normal(jax.random.fold_in(_rk, 1), (1, 128, 256), jnp.float32)
        _lenS = 128 - jax.random.randint(jax.random.fold_in(_rk, 7), (1,), 0, max(1, 128 // 4) + 1, jnp.int32)
        _lenS2 = 12544 - jax.random.randint(jax.random.fold_in(_rk, 8), (1,), 0, max(1, 12544 // 4) + 1, jnp.int32)
        _ctx_1024P = jax.random.normal(jax.random.fold_in(_rk, 11), (1, 16, 256), jnp.float32)
        _ctx_1024c = jax.random.dirichlet(jax.random.fold_in(_rk, 511), 0.3 * jnp.ones((16,), jnp.float32), (1, 12544))
        _ctx_1024t = jnp.einsum('bsk,bkd->bsd', _ctx_1024c, _ctx_1024P)
        _ctx_1024t = _ctx_1024t * jax.lax.rsqrt(jnp.mean(jnp.square(_ctx_1024t)) + 1e-12) * 0.953939
        ctx_1024 = -1.39393e-06 + 0.999914 * (_ctx_1024t + 0.3 * jax.random.normal(jax.random.fold_in(_rk, 611), (1, 12544, 256), jnp.float32))
        return (x, ctx_1024)
    x, ctx_1024 = _rec_inputs()

    def _L0_xattn_setup():
        import jax, jax.numpy as jnp
        import numpy as np
        D_MODEL = 256
        N_HEADS = 16
        HEAD_DIM = D_MODEL // N_HEADS
        B, S = (2, 512)

        def _split_heads(x):
            b, s, _ = x.shape
            return x.reshape(b, s, N_HEADS, HEAD_DIM).transpose(0, 2, 1, 3)
        key = jax.random.key(seed)
        ks = jax.random.split(key, 11)
        scale = 1.0 / np.sqrt(D_MODEL)
        return {'query': jax.random.normal(ks[0], (B, S, D_MODEL), jnp.float32), 'key': jax.random.normal(ks[1], (B, S, D_MODEL), jnp.float32), 'value': jax.random.normal(ks[2], (B, S, D_MODEL), jnp.float32), 'Wq': jax.random.normal(ks[3], (D_MODEL, D_MODEL), jnp.float32) * scale, 'bq': jnp.zeros((D_MODEL,), jnp.float32), 'Wk': jax.random.normal(ks[4], (D_MODEL, D_MODEL), jnp.float32) * scale, 'bk': jnp.zeros((D_MODEL,), jnp.float32), 'Wv': jax.random.normal(ks[5], (D_MODEL, D_MODEL), jnp.float32) * scale, 'bv': jnp.zeros((D_MODEL,), jnp.float32), 'Wo': jax.random.normal(ks[6], (D_MODEL, D_MODEL), jnp.float32) * scale, 'bo': jnp.zeros((D_MODEL,), jnp.float32)}
    _L0_xattn_all = _L0_xattn_setup()
    _L0_xattn_in = {k: v for k, v in _L0_xattn_all.items() if k in ('Wq', 'bq', 'Wk', 'bk', 'Wv', 'bv', 'Wo', 'bo')}
    del _L0_xattn_all

    def _L0_attn_setup():
        import jax, jax.numpy as jnp
        import numpy as np
        from jax import lax
        D_MODEL = 256
        D_INNER = 2 * D_MODEL
        D_CONV = 4
        BATCH = 4
        SEQ = 1024

        def _mixer(x, in_proj_w, in_proj_b, conv_w, conv_b, dt_w, dt_b, b_w, c_w, A_log, D_param, out_w, out_b):
            B, L, _ = x.shape
            xz = jnp.einsum('bld,ed->ble', x, in_proj_w) + in_proj_b
            x_branch, z_branch = jnp.split(xz, 2, axis=-1)
            u = jnp.transpose(x_branch, (0, 2, 1))
            u = lax.conv_general_dilated(u, conv_w, window_strides=(1,), padding=[(D_CONV - 1, 0)], dimension_numbers=('NCH', 'OIH', 'NCH'), feature_group_count=D_INNER) + conv_b[None, :, None]
            u = jnp.transpose(u, (0, 2, 1))
            u = jax.nn.silu(u)
            dt = jax.nn.softplus(jnp.einsum('bld,ed->ble', u, dt_w) + dt_b) + 0.0001
            B_t = jnp.tanh(jnp.einsum('bld,ed->ble', u, b_w))
            C_t = jnp.tanh(jnp.einsum('bld,ed->ble', u, c_w))
            A = jnp.exp(A_log)
            decay = jnp.exp(-dt * A)
            inc = (1.0 - decay) * B_t * u

            def step(state, xs):
                d_t, i_t = xs
                state = d_t * state + i_t
                return (state, state)
            init = jnp.zeros((B, D_INNER), x.dtype)
            _, states = lax.scan(step, init, (jnp.transpose(decay, (1, 0, 2)), jnp.transpose(inc, (1, 0, 2))))
            states = jnp.transpose(states, (1, 0, 2))
            y = C_t * states + D_param * u
            y = y * jax.nn.sigmoid(z_branch)
            return jnp.einsum('ble,de->bld', y, out_w) + out_b
        key = jax.random.key(seed)
        ks = jax.random.split(key, 10)
        s = 0.02
        return {'x': jax.random.normal(ks[0], (BATCH, SEQ, D_MODEL), jnp.float32), 'in_proj_w': jax.random.normal(ks[1], (2 * D_INNER, D_MODEL), jnp.float32) * s, 'in_proj_b': jnp.zeros((2 * D_INNER,), jnp.float32), 'conv_w': jax.random.normal(ks[2], (D_INNER, 1, D_CONV), jnp.float32) * s, 'conv_b': jnp.zeros((D_INNER,), jnp.float32), 'dt_w': jax.random.normal(ks[3], (D_INNER, D_INNER), jnp.float32) * s, 'dt_b': jnp.zeros((D_INNER,), jnp.float32), 'b_w': jax.random.normal(ks[4], (D_INNER, D_INNER), jnp.float32) * s, 'c_w': jax.random.normal(ks[5], (D_INNER, D_INNER), jnp.float32) * s, 'A_log': jax.random.normal(ks[6], (D_INNER,), jnp.float32) * 0.02 - 2.0, 'D_param': jnp.ones((D_INNER,), jnp.float32), 'out_w': jax.random.normal(ks[7], (D_MODEL, D_INNER), jnp.float32) * s, 'out_b': jnp.zeros((D_MODEL,), jnp.float32)}
    _L0_attn_all = _L0_attn_setup()
    _L0_attn_in = {k: v for k, v in _L0_attn_all.items() if k in ('in_proj_w', 'in_proj_b', 'conv_w', 'conv_b', 'dt_w', 'dt_b', 'b_w', 'c_w', 'A_log', 'D_param', 'out_w', 'out_b')}
    del _L0_attn_all

    def _L0_ffn_setup():
        import jax, jax.numpy as jnp
        import numpy as np
        D_MODEL = 256
        EXPANSION = 4
        D_HIDDEN = D_MODEL * EXPANSION
        NUM_STAGES = int(np.log2(D_HIDDEN))

        def butterfly(y, weights, dim):
            lead = y.shape[:-1]
            for stage in range(weights.shape[0]):
                s = 2 ** stage
                nb = dim // (2 * s)
                yr = y.reshape(*lead, nb, 2, s)
                a = yr[..., 0, :]
                b = yr[..., 1, :]
                w = weights[stage].reshape(nb, s, 2, 2)
                na = w[..., 0, 0] * a + w[..., 0, 1] * b
                nb2 = w[..., 1, 0] * a + w[..., 1, 1] * b
                y = jnp.stack([na, nb2], axis=-2).reshape(*lead, dim)
            return y
        key = jax.random.key(seed)
        ks = jax.random.split(key, 6)
        B, S = (4, 512)
        x = jax.random.normal(ks[0], (B, S, D_MODEL), jnp.float32)
        W_exp = jax.random.normal(ks[1], (D_MODEL, D_HIDDEN), jnp.float32) * 0.02
        b_exp = jnp.zeros((D_HIDDEN,), jnp.float32)
        up_weights = jax.random.normal(ks[2], (NUM_STAGES, D_HIDDEN // 2, 2, 2), jnp.float32) * 0.02
        up_bias = jnp.zeros((D_HIDDEN,), jnp.float32)
        down_weights = jax.random.normal(ks[3], (NUM_STAGES, D_HIDDEN // 2, 2, 2), jnp.float32) * 0.02
        W_con = jax.random.normal(ks[4], (D_HIDDEN, D_MODEL), jnp.float32) * 0.02
        b_con = jnp.zeros((D_MODEL,), jnp.float32)
        down_bias = jnp.zeros((D_MODEL,), jnp.float32)
        return dict(x=x, W_exp=W_exp, b_exp=b_exp, up_weights=up_weights, up_bias=up_bias, down_weights=down_weights, W_con=W_con, b_con=b_con, down_bias=down_bias)
    _L0_ffn_all = _L0_ffn_setup()
    _L0_ffn_in = {k: v for k, v in _L0_ffn_all.items() if k in ('W_exp', 'b_exp', 'up_weights', 'up_bias', 'down_weights', 'W_con', 'b_con', 'down_bias')}
    del _L0_ffn_all
    return {'x': x, 'ctx_1024': ctx_1024, 'L0_xattn_Wq': _L0_xattn_in['Wq'], 'L0_xattn_bq': _L0_xattn_in['bq'], 'L0_xattn_Wk': _L0_xattn_in['Wk'], 'L0_xattn_bk': _L0_xattn_in['bk'], 'L0_xattn_Wv': _L0_xattn_in['Wv'], 'L0_xattn_bv': _L0_xattn_in['bv'], 'L0_xattn_Wo': _L0_xattn_in['Wo'], 'L0_xattn_bo': _L0_xattn_in['bo'], 'L0_attn_in_proj_w': _L0_attn_in['in_proj_w'], 'L0_attn_in_proj_b': _L0_attn_in['in_proj_b'], 'L0_attn_conv_w': _L0_attn_in['conv_w'], 'L0_attn_conv_b': _L0_attn_in['conv_b'], 'L0_attn_dt_w': _L0_attn_in['dt_w'], 'L0_attn_dt_b': _L0_attn_in['dt_b'], 'L0_attn_b_w': _L0_attn_in['b_w'], 'L0_attn_c_w': _L0_attn_in['c_w'], 'L0_attn_A_log': _L0_attn_in['A_log'], 'L0_attn_D_param': _L0_attn_in['D_param'], 'L0_attn_out_w': _L0_attn_in['out_w'], 'L0_attn_out_b': _L0_attn_in['out_b'], 'L0_ffn_W_exp': _L0_ffn_in['W_exp'], 'L0_ffn_b_exp': _L0_ffn_in['b_exp'], 'L0_ffn_up_weights': _L0_ffn_in['up_weights'], 'L0_ffn_up_bias': _L0_ffn_in['up_bias'], 'L0_ffn_down_weights': _L0_ffn_in['down_weights'], 'L0_ffn_W_con': _L0_ffn_in['W_con'], 'L0_ffn_b_con': _L0_ffn_in['b_con'], 'L0_ffn_down_bias': _L0_ffn_in['down_bias']}

def reference(x, ctx_1024, L0_xattn_Wq, L0_xattn_bq, L0_xattn_Wk, L0_xattn_bk, L0_xattn_Wv, L0_xattn_bv, L0_xattn_Wo, L0_xattn_bo, L0_attn_in_proj_w, L0_attn_in_proj_b, L0_attn_conv_w, L0_attn_conv_b, L0_attn_dt_w, L0_attn_dt_b, L0_attn_b_w, L0_attn_c_w, L0_attn_A_log, L0_attn_D_param, L0_attn_out_w, L0_attn_out_b, L0_ffn_W_exp, L0_ffn_b_exp, L0_ffn_up_weights, L0_ffn_up_bias, L0_ffn_down_weights, L0_ffn_W_con, L0_ffn_b_con, L0_ffn_down_bias):
    import jax
    import jax.numpy as jnp

    def _L0_xattn_ref(query, key, value, Wq, bq, Wk, bk, Wv, bv, Wo, bo):
        import jax, jax.numpy as jnp
        import numpy as np
        D_MODEL = 256
        N_HEADS = 16
        HEAD_DIM = D_MODEL // N_HEADS
        B, S = (2, 512)

        def _split_heads(x):
            b, s, _ = x.shape
            return x.reshape(b, s, N_HEADS, HEAD_DIM).transpose(0, 2, 1, 3)
        q = _split_heads(query @ Wq.T + bq)
        k = _split_heads(key @ Wk.T + bk)
        v = _split_heads(value @ Wv.T + bv)
        energy = jnp.einsum('bhqd,bhkd->bhqk', q, k) / jnp.sqrt(jnp.asarray(HEAD_DIM, q.dtype))
        attn = jax.nn.softmax(energy, axis=-1)
        x = jnp.einsum('bhqk,bhkd->bhqd', attn, v)
        x = x.transpose(0, 2, 1, 3).reshape(query.shape[0], -1, D_MODEL)
        return x @ Wo.T + bo

    def _L0_attn_ref(x, in_proj_w, in_proj_b, conv_w, conv_b, dt_w, dt_b, b_w, c_w, A_log, D_param, out_w, out_b):
        import jax, jax.numpy as jnp
        import numpy as np
        from jax import lax
        D_MODEL = 256
        D_INNER = 2 * D_MODEL
        D_CONV = 4
        BATCH = 4
        SEQ = 1024

        def _mixer(x, in_proj_w, in_proj_b, conv_w, conv_b, dt_w, dt_b, b_w, c_w, A_log, D_param, out_w, out_b):
            B, L, _ = x.shape
            xz = jnp.einsum('bld,ed->ble', x, in_proj_w) + in_proj_b
            x_branch, z_branch = jnp.split(xz, 2, axis=-1)
            u = jnp.transpose(x_branch, (0, 2, 1))
            u = lax.conv_general_dilated(u, conv_w, window_strides=(1,), padding=[(D_CONV - 1, 0)], dimension_numbers=('NCH', 'OIH', 'NCH'), feature_group_count=D_INNER) + conv_b[None, :, None]
            u = jnp.transpose(u, (0, 2, 1))
            u = jax.nn.silu(u)
            dt = jax.nn.softplus(jnp.einsum('bld,ed->ble', u, dt_w) + dt_b) + 0.0001
            B_t = jnp.tanh(jnp.einsum('bld,ed->ble', u, b_w))
            C_t = jnp.tanh(jnp.einsum('bld,ed->ble', u, c_w))
            A = jnp.exp(A_log)
            decay = jnp.exp(-dt * A)
            inc = (1.0 - decay) * B_t * u

            def step(state, xs):
                d_t, i_t = xs
                state = d_t * state + i_t
                return (state, state)
            init = jnp.zeros((B, D_INNER), x.dtype)
            _, states = lax.scan(step, init, (jnp.transpose(decay, (1, 0, 2)), jnp.transpose(inc, (1, 0, 2))))
            states = jnp.transpose(states, (1, 0, 2))
            y = C_t * states + D_param * u
            y = y * jax.nn.sigmoid(z_branch)
            return jnp.einsum('ble,de->bld', y, out_w) + out_b
        return _mixer(x, in_proj_w, in_proj_b, conv_w, conv_b, dt_w, dt_b, b_w, c_w, A_log, D_param, out_w, out_b)

    def _L0_ffn_ref(x, W_exp, b_exp, up_weights, up_bias, down_weights, W_con, b_con, down_bias):
        import jax, jax.numpy as jnp
        import numpy as np
        D_MODEL = 256
        EXPANSION = 4
        D_HIDDEN = D_MODEL * EXPANSION
        NUM_STAGES = int(np.log2(D_HIDDEN))

        def butterfly(y, weights, dim):
            lead = y.shape[:-1]
            for stage in range(weights.shape[0]):
                s = 2 ** stage
                nb = dim // (2 * s)
                yr = y.reshape(*lead, nb, 2, s)
                a = yr[..., 0, :]
                b = yr[..., 1, :]
                w = weights[stage].reshape(nb, s, 2, 2)
                na = w[..., 0, 0] * a + w[..., 0, 1] * b
                nb2 = w[..., 1, 0] * a + w[..., 1, 1] * b
                y = jnp.stack([na, nb2], axis=-2).reshape(*lead, dim)
            return y
        h = jnp.einsum('bsd,dh->bsh', x, W_exp) + b_exp
        h = butterfly(h, up_weights, D_HIDDEN)
        h = jax.nn.gelu(h + up_bias, approximate=False)
        h = butterfly(h, down_weights, D_HIDDEN)
        y = jnp.einsum('bsh,hd->bsd', h, W_con) + b_con
        return y + down_bias
    x = x + _L0_xattn_ref(_layernorm(x, axis=-1), ctx_1024, ctx_1024, L0_xattn_Wq, L0_xattn_bq, L0_xattn_Wk, L0_xattn_bk, L0_xattn_Wv, L0_xattn_bv, L0_xattn_Wo, L0_xattn_bo)
    x = x + _L0_attn_ref(_layernorm(x, axis=-1), L0_attn_in_proj_w, L0_attn_in_proj_b, L0_attn_conv_w, L0_attn_conv_b, L0_attn_dt_w, L0_attn_dt_b, L0_attn_b_w, L0_attn_c_w, L0_attn_A_log, L0_attn_D_param, L0_attn_out_w, L0_attn_out_b)
    x = x + _L0_ffn_ref(_layernorm(x, axis=-1), L0_ffn_W_exp, L0_ffn_b_exp, L0_ffn_up_weights, L0_ffn_up_bias, L0_ffn_down_weights, L0_ffn_W_con, L0_ffn_b_con, L0_ffn_down_bias)
    return x

_drawn_inputs = setup_inputs


def setup_inputs(seed=0):
    import zlib

    import numpy as np

    out = dict(_drawn_inputs(seed))
    spreads = {'L0_xattn_bq': (0.0, 0.422),
     'L0_xattn_bk': (0.0, 2.0),
     'L0_xattn_bv': (0.0, 0.1),
     'L0_xattn_bo': (0.0, 0.1),
     'L0_attn_in_proj_b': (0.0, 0.8),
     'L0_attn_conv_b': (0.0, 0.8),
     'L0_attn_dt_b': (0.0, 2.0),
     'L0_attn_D_param': (1.0, 0.6),
     'L0_attn_out_b': (0.0, 0.1),
     'L0_ffn_b_exp': (0.0, 0.1),
     'L0_ffn_up_bias': (0.0, 0.1),
     'L0_ffn_b_con': (0.0, 0.1),
     'L0_ffn_down_bias': (0.0, 0.1)}
    factors = {'L0_attn_in_proj_w': 8.0,
     'L0_attn_conv_w': 8.0,
     'L0_attn_dt_w': 64.0,
     'L0_attn_b_w': 64.0,
     'L0_attn_c_w': 64.0,
     'L0_attn_A_log': 64.0,
     'L0_attn_out_w': 5.219}
    for name, (base, spread) in spreads.items():
        noise = np.random.default_rng([zlib.crc32(name.encode()), seed]).standard_normal(out[name].shape)
        drawn = base * np.exp(spread * noise) if base else spread * noise
        out[name] = jnp.asarray(drawn.astype(out[name].dtype))
    for name, factor in factors.items():
        out[name] = (out[name] * factor).astype(out[name].dtype)
    return out
```

```python
from contextlib import ExitStack

import concourse.bass as bass
from concourse import mybir

F32 = mybir.dt.float32
F32R = mybir.dt.float32r
ALU = mybir.AluOpType
ACT = mybir.ActivationFunctionType
AX_X = mybir.AxisListType.X

P = 128
D = 256
DC = D // P
NQ = 128
NK = 12544
H = 16
DH = D // H
TK = 128
CT = 2
CK = TK * CT
NCH = NK // CK
GP = 4
VW = 32
STACK = 3
K_COPIES = 2 * GP
ONE_ROW = 32 * STACK
INNER = 512
IC = INNER // P
TAPS = 4
HID = 1024
HC = HID // P
STAGES = 10
LN_EPS = 1e-5
SUM_LIMIT = 1e30
assert NCH * CK == NK and NCH % 2 == 1 and H * DH == D and 4 * 32 == P


def perceiver_block(nc: bass.Bass, A):
    with ExitStack() as ctx:
        def sb(name, shape, dt=F32):
            return ctx.enter_context(nc.sbuf_tensor(name, shape, dt))

        def pb(name, shape, dt=F32):
            return ctx.enter_context(nc.psum_tensor(name, shape, dt))

        def sem(name):
            return ctx.enter_context(nc.semaphore(name))

        ident = sb("ident", [P, P])
        side = sb("side", [P, 2])
        x_tok = sb("x_tok", [P, D])
        xn_tok = sb("xn_tok", [P, D])
        xn_T = sb("xn_T", [P, DC, NQ])
        stats = sb("stats", [P, 6])
        mv = sb("mv", [P, 2])
        var, std, rstd, newton = (sb(n, [P, 1]) for n in ("var", "std", "rstd", "newton"))
        wq = sb("wq", [P, DC, D])
        wk = sb("wk", [P, DC, D])
        wv = sb("wv", [P, DC, D])
        wo = sb("wo", [P, DC, D])
        wk_hi = sb("wk_hi", [P, DC, D], F32R)
        wk_lo = sb("wk_lo", [P, DC, D], F32R)
        wv_hi = sb("wv_hi", [P, DC, D], F32R)
        wv_lo = sb("wv_lo", [P, DC, D], F32R)
        bq = sb("bq", [P, 2])
        bk = sb("bk", [P, 2])
        bv2 = sb("bv2", [P, CT, D])
        bo = sb("bo", [P, D])
        q_T = sb("q_T", [P, 2, NQ])
        q_hi = sb("q_hi", [P, 2, 2, NQ], F32R)
        q_lo = sb("q_lo", [P, 2, 2, NQ], F32R)
        q_stack = sb("q_stack", [P, 2, GP, 2, NQ], F32R)
        raw = [sb(f"raw{i}", [P, DC, CK]) for i in range(2)]
        c_hi = [sb(f"c_hi{i}", [P, DC, CK], F32R) for i in range(2)]
        c_lo = [sb(f"c_lo{i}", [P, DC, CK], F32R) for i in range(2)]
        k_hi = [sb(f"k_hi{i}", [P, 2, CK], F32R) for i in range(2)]
        k_stack = [sb(f"k_stack{i}", [P, 2, GP, CK], F32R) for i in range(2)]
        v_sb = [sb(f"v_sb{i}", [P, CT, H, VW]) for i in range(2)]
        probs = [sb(f"probs{i}", [P, 8, NQ]) for i in range(4)]
        mx = sb("mx", [P, H])
        neg_max = sb("neg_max", [H, NQ], F32R)
        acc_sb = sb("acc_sb", [P, 4, NQ])
        r_sum = sb("r_sum", [P, H])
        attn = sb("attn", [P, D])
        attn_T = sb("attn_T", [P, DC, NQ])
        x_bo = sb("x_bo", [P, D])
        x1 = sb("x1", [P, D])
        ok = sb("ok", [P, H])
        ok_row = sb("ok_row", [P, 1])
        ok_all = sb("ok_all", [1, 1])
        ok_flag = sb("ok_flag", [1, 1], mybir.dt.int32)

        in_w = sb("in_w", [P, DC, 2 * INNER])
        in_b = sb("in_b", [P, 2 * IC])
        conv_w = sb("conv_w", [P, IC, TAPS])
        conv_b = sb("conv_b", [P, IC])
        dt_w = sb("dt_w", [P, IC, INNER])
        b_w = sb("b_w", [P, IC, INNER])
        c_w = sb("c_w", [P, IC, INNER])
        dt_b = sb("dt_b", [P, IC])
        a_log = sb("a_log", [P, IC])
        neg_a = sb("neg_a", [P, IC])
        d_par = sb("d_par", [P, IC])
        out_w = sb("out_w", [P, IC, D])
        out_b = sb("out_b", [P, D])
        xb = sb("xb", [P, IC, TAPS - 1 + NQ])
        z = sb("z", [P, IC, NQ])
        u = sb("u", [P, IC, NQ])
        (z_exp, z_sig, conv, c_exp, d_u, dt_x, dt_a, dt_e) = (
            probs[i // 2][:, i % 2 * IC:(i % 2 + 1) * IC, :] for i in range(8))
        (b_t, c_t, decay, states, y_mix) = (
            sb(n, [P, IC, NQ]) for n in ("b_t", "c_t", "decay", "states", "y_mix"))
        x2 = sb("x2", [P, D])

        up_y = [sb(f"up_y{i}", [P, HID]) for i in range(2)]
        up_yb = sb("up_yb", [1, HID])
        down_y = [sb(f"down_y{i}", [P, HID]) for i in range(2)]
        prod = [sb(f"prod{i}", [P, HID]) for i in range(2)]
        stage_w = [sb(f"stage_w{i}", [P, 2, HID]) for i in range(2)]
        e_con = [t[:, :, :, :].rearrange("p t h c -> p (t h c)").rearrange("p (m d) -> p m d", d=D) for t in v_sb]
        up_bias = sb("up_bias", [P, HC])
        ones_row = sb("ones_row", [1, NQ])
        out_bias = sb("out_bias", [P, 2, D])
        h_pre, gelu = probs[0], probs[1]
        y_out = sb("y_out", [P, D])

        acc = pb("acc", [P, 4, NQ])
        scores = [pb(f"scores{i}", [P, 2 * 512]) for i in range(2)]
        k_ps = [pb(f"k_ps{i}", [P, 2, CK]) for i in range(2)]
        v_ps = pb("v_ps", [P, CT, D])

        x_in, consts_in, wq_in, wk_in, wv_in, wo_in, mixer_in, ffn_in = (sem(n) for n in (
            "x_in", "consts_in", "wq_in", "wk_in", "wv_in", "wo_in", "mixer_in", "ffn_in"))
        raw_in = [sem("raw_in0"), sem("raw_in1")]
        stacked = [sem("stacked0"), sem("stacked1")]
        wk_split, wv_split = sem("wk_split"), sem("wv_split")
        split_hi, split = sem("split_hi"), sem("split")
        k_done, v_done = sem("k_done"), sem("v_done")
        k_hi_done, k_lo_done = sem("k_hi_done"), sem("k_lo_done")
        v_ready = sem("v_ready")
        scored, exped, weighed = sem("scored"), sem("exped"), sem("weighed")
        pool_const = sem("pool_const")
        xn_ready, xn_turned, xn_T_ready = sem("xn_ready"), sem("xn_turned"), sem("xn_T_ready")
        var_ready, std_ready = sem("var_ready"), sem("std_ready")
        q_done, q_ready, q_stacked = sem("q_done"), sem("q_ready"), sem("q_stacked")
        max_scored, max_read, max_turned, shift_ready, shift_in = (sem(n) for n in (
            "max_scored", "max_read", "max_turned", "shift_ready", "shift_in"))
        acc_copied, acc_turned, attn_ready, attn_turned, attn_T_ready, wo_done, x1_ready = (sem(n) for n in (
            "acc_copied", "acc_turned", "attn_ready", "attn_turned", "attn_T_ready", "wo_done", "x1_ready"))
        in_done_x, in_done_z, conv_ready, conv_exped, z_ready, z_exped, u_ready = (sem(n) for n in (
            "in_done_x", "in_done_z", "conv_ready", "conv_exped", "z_ready", "z_exped", "u_ready"))
        dt_done, b_done, c_done, dt_abs, dt_log, dt_arg, decay_ready, b_ready, c_ready, neg_a_ready = (
            sem(n) for n in ("dt_done", "b_done", "c_done", "dt_abs", "dt_log", "dt_arg", "decay_ready",
                             "b_ready", "c_ready", "neg_a_ready"))
        y_ready, out_proj_done, h_done, h_ready, gelu_ready, con_done, y_out_ready, out_written = (
            sem(n) for n in ("y_ready", "out_proj_done", "h_done", "h_ready", "gelu_ready", "con_done",
                             "y_out_ready", "out_written"))
        stage_in = [sem("stage_in0"), sem("stage_in1")]
        ok_ready, ok_turned, ok_known = sem("ok_ready"), sem("ok_turned"), sem("ok_known")
        (g_raw, g_hi, g_split, g_k, g_k_hi, g_k_copied, g_k_lo, g_scored, g_read, g_v, g_v_ready, g_exped,
         g_weighed, g_turned, g_shift, g_shift_in, g_zeroed, g_acc_copied, g_acc_turned, g_attn,
         g_attn_turned, g_attn_T, g_wo_done, g_maxed) = (sem("g_" + n) for n in (
             "raw", "hi", "split", "k", "k_hi", "k_copied", "k_lo", "scored", "read", "v", "v_ready", "exped",
             "weighed", "turned", "shift", "shift_in", "zeroed", "acc_copied", "acc_turned", "attn",
             "attn_turned", "attn_T", "wo_done", "maxed"))
        g_step = sem("g_step")
        butterfly = sem("butterfly")
        rows_in = sem("rows_in")
        butterflies_done = sem("butterflies_done")
        e_turned, e_copied = sem("e_turned"), sem("e_copied")
        dve_step, act_step = sem("dve_step"), sem("act_step")

        def row_on_all(name):
            return A[name].partition_broadcast(P)

        def per_channel(tile, n, width):
            return tile[:, 0:n].unsqueeze(2).broadcast_to([P, n, width])

        block = ctx.enter_context(nc.Block())
        LAST = NCH - 1

        class Chunk:

            def __init__(self, c, par, nth, number=None):
                self.c, self.par, self.nth, self.number = c, par, nth, number

            def later(self, n):
                return Chunk(self.c + n, (self.par + n) % 2, self.nth + (n + self.par) // 2,
                             None if self.number is None else self.number + n)

            def has(self, n):
                return self.number is None or self.number + n <= LAST

        def peeled(c):
            return Chunk(c, c % 2, c // 2 + 1, c)

        def over_chunks(eng, step):
            step(peeled(0))
            with eng.Fori(0, (NCH - 5) // 2) as n:
                step(Chunk(2 * n + 1, 1, n + 1))
                step(Chunk(2 * n + 2, 0, n + 2))
            for c in range(NCH - 4, NCH):
                step(peeled(c))

        def wait_from(eng, s, value, k, first):
            if k.number is None or k.number >= first:
                eng.wait_ge(s, value)

        def unless_ok(eng, general):
            eng.wait_ge(ok_known, 1)
            good = eng.value_load(ok_flag[0:1, 0:1], min_val=0, max_val=1)
            with eng.If(good == 0):
                general()
            with eng.Else():
                eng.nop()

        @block.sync
        def _(sp):
            def load_context(k):
                wait_from(sp, split, k.c - 1, k, 2)
                sp.dma_start(raw[k.par][:, :, :],
                             A["ctx"][bass.ds(k.c, 1), :, :, :].rearrange("c p k n -> (c p) k n")
                             ).then_inc(raw_in[k.par], 16)

            def copy_k_hi(par, copied):
                for r in range(2):
                    for j in range(GP):
                        sp.dma_start(k_stack[par][32 * r:32 * r + 32, :, j, :].bitcast(F32),
                                     k_hi[par][32 * j:32 * j + 32, :, :].bitcast(F32)).then_inc(copied, 16)

            def load_shift(landed):
                sp.dma_start(q_stack[ONE_ROW:ONE_ROW + 1, :, :, :, :].rearrange("o g j s q -> o (g j s q)")
                             .bitcast(F32), neg_max[:, :].bitcast(F32)).then_inc(landed, 16)

            def stack_k(k):
                sp.wait_ge(k_hi_done, k.c + 1)
                wait_from(sp, scored, 4 * k.c - 4, k, 2)
                copy_k_hi(k.par, stacked[k.par])

            sp.dma_start(x_tok[:, :], A["x"][0]).then_inc(x_in, 16)
            sp.dma_start(ident[:, :], A["ident"]).then_inc(consts_in, 16)
            sp.dma_start(wk[:, :, :], A["wk"]).then_inc(wk_in, 16)
            load_context(peeled(0))
            sp.dma_start(bk[:, :], A["bk"]).then_inc(wk_in, 16)
            sp.dma_start(side[:, :], A["side"]).then_inc(consts_in, 16)
            sp.dma_start(wq[:, :, :], A["wq"]).then_inc(wq_in, 16)
            sp.dma_start(bq[:, :], A["bq"]).then_inc(wq_in, 16)
            load_context(peeled(1))
            sp.dma_start(wv[:, :, :], A["wv"]).then_inc(wv_in, 16)
            for t in range(CT):
                sp.dma_start(bv2[:, t, :], row_on_all("bv")).then_inc(wv_in, 16)

            sp.wait_ge(q_ready, 4)
            for r, part in enumerate((q_hi, q_lo, q_hi)):
                for j in range(GP):
                    sp.dma_start(q_stack[32 * r:32 * r + 32, :, j, :, :].bitcast(F32),
                                 part[32 * j:32 * j + 32, :, :, :].bitcast(F32)).then_inc(q_stacked, 16)
            stack_k(peeled(0))
            stack_k(peeled(1))
            load_context(peeled(2))
            load_context(peeled(3))

            sp.dma_start(wo[:, :, :], A["wo"]).then_inc(wo_in, 16)
            sp.dma_start(bo[:, :], row_on_all("bo")).then_inc(wo_in, 16)
            for to, name in ((in_w, "in_w"), (dt_w, "dt_w"), (b_w, "b_w"), (c_w, "c_w"),
                             (out_w, "out_w"), (conv_w, "conv_w")):
                sp.dma_start(to[:, :, :], A[name]).then_inc(mixer_in, 16)
            for to, name in ((in_b, "in_b"), (conv_b, "conv_b"), (dt_b, "dt_b"), (a_log, "a_log"),
                             (d_par, "d_par")):
                sp.dma_start(to[:, :], A[name]).then_inc(mixer_in, 16)
            sp.dma_start(out_b[:, :], row_on_all("out_b")).then_inc(mixer_in, 16)
            sp.dma_start(up_bias[:, :], A["up_bias"]).then_inc(ffn_in, 16)
            sp.dma_start(out_bias[:, 0, :], row_on_all("b_con")).then_inc(ffn_in, 16)
            sp.dma_start(out_bias[:, 1, :], row_on_all("down_bias")).then_inc(ffn_in, 16)

            sp.wait_ge(pool_const, 1)
            sp.wait_ge(shift_ready, 1)
            load_shift(shift_in)

            def step(k):
                if k.has(4):
                    load_context(k.later(4))
                if k.has(2):
                    stack_k(k.later(2))

            over_chunks(sp, step)

            def general():
                def load(n):
                    sp.dma_start(raw[0][:, :, :],
                                 A["ctx"][bass.ds(n, 1), :, :, :].rearrange("c p k n -> (c p) k n")
                                 ).then_inc(g_raw, 16)

                def sweep(before):
                    load(0)
                    with sp.Fori(0, NCH - 1) as n:
                        sp.wait_ge(g_k_hi, n + (before + 1))
                        copy_k_hi(0, g_k_copied)
                        load(n + 1)
                    sp.wait_ge(g_k_hi, before + NCH)
                    copy_k_hi(0, g_k_copied)

                sweep(0)
                sp.wait_ge(g_shift, 1)
                load_shift(g_shift_in)
                sweep(NCH)

            unless_ok(sp, general)
            sp.wait_ge(y_out_ready, 1)
            sp.dma_start(A["out"][0], y_out[:, :]).then_inc(out_written, 16)
            sp.wait_ge(out_written, 16)

        @block.tensor
        def _(pe):
            def times_wk(par):
                terms = ((wk_hi, c_hi), (wk_lo, c_hi), (wk_hi, c_lo))
                for g in range(2):
                    n = 0
                    for w, c in terms:
                        for kc in range(DC):
                            last = pe.matmul(k_ps[par][:, g, :], w[:, kc, g * P:(g + 1) * P],
                                             c[par][:, kc, :], start=(n == 0), stop=(n == 5))
                            n += 1
                return last

            def project_k(k):
                pe.wait_ge(split, k.c + 1)
                wait_from(pe, k_lo_done, k.c - 1, k, 2)
                times_wk(k.par).then_inc(k_done, 1)

            def times_wv(par):
                terms = ((c_hi, wv_hi), (c_hi, wv_lo), (c_lo, wv_hi))
                for t in range(CT):
                    n = 0
                    for c, w in terms:
                        for kc in range(DC):
                            last = pe.matmul(v_ps[:, t, :], c[par][:, kc, t * TK:(t + 1) * TK],
                                             w[:, kc, :], start=(n == 0), stop=(n == 5))
                            n += 1
                return last

            def project_v(k):
                pe.wait_ge(split, k.c + 1)
                wait_from(pe, v_ready, k.c, k, 1)
                times_wv(k.par).then_inc(v_done, 1)

            def times_q(par, i):
                t, g = i // 2, i % 2
                for j in range(GP):
                    last = pe.matmul(scores[i % 2][:, j * 2 * NQ:(j + 1) * 2 * NQ],
                                     k_stack[par][:, g, j, t * TK:(t + 1) * TK],
                                     q_stack[:, g, j, :, :], start=True, stop=True)
                return last

            def score(k, i):
                if i == 0:
                    pe.wait_ge(stacked[k.par], 16 * K_COPIES * k.nth)
                    pe.wait_ge(k_lo_done, k.c + 1)
                times_q(k.par, i).then_inc(scored, 1)

            def times_probs(par, i, begin=False):
                t, g = i // 2, i % 2
                for h in range(8):
                    last = pe.matmul(acc[32 * (h % 4):32 * (h % 4) + VW, 2 * g + h // 4, :],
                                     v_sb[par][:, t, 8 * g + h, :], probs[i][:, h, :],
                                     start=(begin and h < 4), stop=False, skip_group_check=True)
                return last

            def weigh(k, i, begin=False):
                times_probs(k.par, i, begin).then_inc(weighed, 1)

            def scores_by_query(b):
                for i in range(4):
                    g, j, s = b // 2, 2 * (b % 2) + i // 2, i % 2
                    last = pe.matmul(scores[b % 2][:, i * CK:(i + 1) * CK], q_stack[0:ONE_ROW, g, j, s, :],
                                     k_stack[0][0:ONE_ROW, g, j, :], start=True, stop=True)
                return last

            def out_attention(copied, turned, ready, a_turned, a_ready, done, between=lambda: None):
                pe.wait_ge(copied, 1)
                for b in range(4):
                    last = pe.transpose(scores[0][:, b * P:(b + 1) * P], acc_sb[:, b, :], ident[:, :])
                last.then_inc(turned, 1)
                pe.wait_ge(ready, 1)
                for kc in range(DC):
                    last = pe.transpose(scores[1][:, kc * NQ:(kc + 1) * NQ], attn[:, kc * P:(kc + 1) * P],
                                        ident[:, :])
                last.then_inc(a_turned, 1)
                between()
                pe.wait_ge(a_ready, 1)
                pe.wait_ge(wo_in, 32)
                for kc in range(DC):
                    last = pe.matmul(v_ps[:, 0, :], attn_T[:, kc, :], wo[:, kc, :],
                                     start=(kc == 0), stop=(kc == DC - 1))
                last.then_inc(done, 1)

            pe.wait_ge(wk_split, 1)
            project_k(peeled(0))
            pe.wait_ge(consts_in, 32)

            def turn_normed(nth, to):
                pe.wait_ge(xn_ready, nth)
                for kc in range(DC):
                    last = pe.transpose(to[:, kc * NQ:(kc + 1) * NQ], xn_tok[:, kc * P:(kc + 1) * P],
                                        ident[:, :])
                last.then_inc(xn_turned, 1)
                pe.wait_ge(xn_T_ready, nth)

            turn_normed(1, scores[0])
            pe.wait_ge(wq_in, 32)
            for g in range(2):
                for kc in range(DC):
                    last = pe.matmul(scores[1][:, g * NQ:(g + 1) * NQ], wq[:, kc, g * P:(g + 1) * P],
                                     xn_T[:, kc, :], start=(kc == 0), stop=(kc == DC - 1))
            last.then_inc(q_done, 1)
            pe.wait_ge(wv_split, 1)
            project_v(peeled(0))
            project_k(peeled(1))

            pe.wait_ge(q_stacked, 16 * STACK * GP)
            pe.wait_ge(stacked[0], 16 * K_COPIES)
            pe.wait_ge(k_lo_done, 1)
            for b in range(4):
                if b >= 2:
                    pe.wait_ge(max_read, b - 1)
                scores_by_query(b).then_inc(max_scored, 1)
            pe.wait_ge(max_read, 4)
            pe.transpose(acc[0:H, 0, :], mx[:, :], ident[:, :]).then_inc(max_turned, 1)

            pe.wait_ge(shift_in, 16)
            pe.wait_ge(pool_const, 1)

            def step(k):
                if k.has(1):
                    project_v(k.later(1))
                for i in range(4):
                    if k.number != 0 or i >= 2:
                        pe.wait_ge(exped, 4 * k.c + i - 1)
                    score(k, i)
                    if i < 2:
                        if k.number != 0:
                            weigh(k.later(1), i + 2)
                    else:
                        if i == 2:
                            pe.wait_ge(v_ready, k.c + 1)
                        weigh(k, i - 2, begin=(k.number == 0 and i == 2))
                    if i == 1 and k.has(2):
                        project_k(k.later(2))

            over_chunks(pe, step)
            for i in (2, 3):
                pe.wait_ge(exped, 4 * LAST + i + 1)
                weigh(peeled(LAST), i)

            def turn_ok():
                pe.wait_ge(ok_ready, 1)
                pe.transpose(scores[1][0:1, 512:512 + P], ok_row[:, :], ident[:, :]).then_inc(ok_turned, 1)

            out_attention(acc_copied, acc_turned, attn_ready, attn_turned, attn_T_ready, wo_done, turn_ok)

            def general():
                with pe.Fori(0, NCH) as n:
                    pe.wait_ge(g_split, n + 1)
                    times_wk(0).then_inc(g_k, 1)
                    pe.wait_ge(g_k_copied, 16 * K_COPIES * n + 16 * K_COPIES)
                    pe.wait_ge(g_k_lo, n + 1)
                    for b in range(4):
                        if b >= 2:
                            pe.wait_ge(g_read, 4 * n + (b - 1))
                        scores_by_query(b).then_inc(g_scored, 1)
                pe.wait_ge(g_read, 4 * NCH)
                pe.transpose(acc[0:H, 0, :], mx[:, :], ident[:, :]).then_inc(g_turned, 1)
                pe.wait_ge(g_shift_in, 16)
                pe.wait_ge(g_zeroed, 1)
                with pe.Fori(0, NCH) as n:
                    pe.wait_ge(g_split, n + (NCH + 1))
                    times_wk(0).then_inc(g_k, 1)
                    times_wv(0).then_inc(g_v, 1)
                    pe.wait_ge(g_k_copied, 16 * K_COPIES * n + 16 * K_COPIES * (NCH + 1))
                    pe.wait_ge(g_k_lo, n + (NCH + 1))
                    pe.wait_ge(g_v_ready, n + 1)
                    for i in range(4):
                        times_q(0, i).then_inc(g_scored, 1)
                        pe.wait_ge(g_exped, 4 * n + (i + 1))
                        times_probs(0, i).then_inc(g_weighed, 1)
                out_attention(g_acc_copied, g_acc_turned, g_attn, g_attn_turned, g_attn_T, g_wo_done)

            unless_ok(pe, general)

            turn_normed(2, scores[1])
            pe.wait_ge(mixer_in, 16 * 12)
            for e in range(2 * IC):
                for kc in range(DC):
                    last = pe.matmul(scores[0][:, e * NQ:(e + 1) * NQ], in_w[:, kc, e * P:(e + 1) * P],
                                     xn_T[:, kc, :], start=(kc == 0), stop=(kc == DC - 1))
                if e == IC - 1:
                    last.then_inc(in_done_x, 1)
            last.then_inc(in_done_z, 1)

            pe.wait_ge(butterflies_done, 1)
            for b in range(4):
                if b >= 2:
                    pe.wait_ge(e_copied, b - 1)
                for i in range(4):
                    m, s = 2 * b + i // 2, i % 2
                    last = pe.transpose(k_ps[b % 2][:, i // 2, s * P:(s + 1) * P],
                                        down_y[s][:, m * P:(m + 1) * P], ident[:, :])
                last.then_inc(e_turned, 1)

            pe.wait_ge(u_ready, 1)
            for w, to, done in ((dt_w, scores[1][:, 0:512], dt_done), (b_w, scores[1][:, 512:1024], b_done),
                                (c_w, v_ps[:, :, :].rearrange("p t n -> p (t n)"), c_done)):
                for e in range(IC):
                    for kc in range(IC):
                        last = pe.matmul(to[:, e * NQ:(e + 1) * NQ], w[:, kc, e * P:(e + 1) * P],
                                         u[:, kc, :], start=(kc == 0), stop=(kc == IC - 1))
                last.then_inc(done, 1)
            pe.wait_ge(y_ready, 1)
            for kc in range(IC):
                last = pe.matmul(k_ps[0][:, 0, :], y_mix[:, kc, :], out_w[:, kc, :],
                                 start=(kc == 0), stop=(kc == IC - 1))
            last.then_inc(out_proj_done, 1)

            turn_normed(3, scores[1])
            for m in range(HC):
                for kc in range(DC):
                    pe.matmul(scores[0][:, m * NQ:(m + 1) * NQ], up_y[kc][:, m * P:(m + 1) * P],
                              xn_T[:, kc, :], start=(kc == 0), stop=False)
                last = pe.matmul(scores[0][:, m * NQ:(m + 1) * NQ], up_yb[0:1, m * P:(m + 1) * P],
                                 ones_row[0:1, :], start=False, stop=True)
            last.then_inc(h_done, 1)
            pe.wait_ge(gelu_ready, 1)
            pe.wait_ge(e_copied, 4)
            for m in range(HC):
                last = pe.matmul(k_ps[1][:, 0, :], gelu[:, m, :], e_con[m // 4][:, m % 4, :],
                                 start=(m == 0), stop=(m == HC - 1))
            last.then_inc(con_done, 1)

        @block.scalar
        def _(act):
            def round_k(par):
                for g in range(2):
                    last = act.activation(k_hi[par][:, g, :], k_ps[par][:, g, :], ACT.Identity,
                                          bias=bk[:, g:g + 1])
                return last

            def k_high(k):
                act.wait_ge(k_done, k.c + 1)
                wait_from(act, stacked[k.par], 16 * K_COPIES * (k.nth - 1), k, 2)
                round_k(k.par).then_inc(k_hi_done, 1)

            def exp_scores(i):
                return act.activation(probs[i][:, :, :].rearrange("p h q -> p (h q)"), scores[i % 2][:, :],
                                      ACT.Exp, scale=DH ** -0.5)

            def negate_maxima():
                return act.activation(neg_max[:, :], acc[0:H, 0, :], ACT.Copy, scale=-1.0)

            def root(nth):
                act.wait_ge(var_ready, nth)
                act.activation(std[:, :], var[:, :], ACT.Sqrt).then_inc(std_ready, 1)

            root(1)
            act.wait_ge(wk_in, 32)
            k_high(peeled(0))
            k_high(peeled(1))
            act.wait_ge(max_turned, 1)
            negate_maxima().then_inc(shift_ready, 1)

            def step(k):
                for i in range(4):
                    act.wait_ge(scored, 4 * k.c + i + 1)
                    if k.number != 0:
                        act.wait_ge(weighed, 4 * k.c + i - 3)
                    exp_scores(i).then_inc(exped, 1)
                    if i == 1 and k.has(2):
                        k_high(k.later(2))

            over_chunks(act, step)
            act.wait_ge(weighed, 4 * NCH)
            act.activation(acc_sb[:, :, :], acc[:, :, :], ACT.Copy).then_inc(acc_copied, 1)

            def general():
                with act.Fori(0, NCH) as n:
                    act.wait_ge(g_k, n + 1)
                    round_k(0).then_inc(g_k_hi, 1)
                act.wait_ge(g_turned, 1)
                negate_maxima().then_inc(g_shift, 1)
                with act.Fori(0, NCH) as n:
                    act.wait_ge(g_k, n + (NCH + 1))
                    round_k(0).then_inc(g_k_hi, 1)
                    for i in range(4):
                        act.wait_ge(g_scored, 4 * n + (4 * NCH + i + 1))
                        exp_scores(i).then_inc(g_exped, 1)
                act.wait_ge(g_weighed, 4 * NCH)
                act.activation(acc_sb[:, :, :], acc[:, :, :], ACT.Copy).then_inc(g_acc_copied, 1)

            unless_ok(act, general)

            root(2)
            act.wait_ge(mixer_in, 16 * 12)
            act.activation(neg_a[:, :], a_log[:, :], ACT.Exp).then_inc(act_step, 1)
            act.wait_ge(act_step, 1)
            act.activation(neg_a[:, :], neg_a[:, :], ACT.Copy, scale=-1.0).then_inc(neg_a_ready, 1)
            act.wait_ge(in_done_z, 1)
            for e in range(IC):
                last = act.activation(z[:, e, :], scores[0][:, (IC + e) * NQ:(IC + e + 1) * NQ], ACT.Identity,
                                      bias=in_b[:, IC + e:IC + e + 1])
            last.then_inc(z_ready, 1)
            act.wait_ge(z_ready, 1)
            act.activation(z_exp[:, :, :], z[:, :, :], ACT.Exp, scale=-1.0).then_inc(z_exped, 1)
            act.wait_ge(conv_ready, 1)
            act.activation(c_exp[:, :, :], conv[:, :, :], ACT.Exp, scale=-1.0).then_inc(conv_exped, 1)
            for b in range(4):
                act.wait_ge(e_turned, b + 1)
                act.activation(e_con[b // 2][:, 2 * (b % 2):2 * (b % 2) + 2, :], k_ps[b % 2][:, :, :], ACT.Copy).then_inc(e_copied, 1)
            act.wait_ge(b_done, 1)
            act.activation(b_t[:, :, :].rearrange("p e n -> p (e n)"), scores[1][:, 512:1024],
                           ACT.Tanh).then_inc(b_ready, 1)
            act.wait_ge(dt_abs, 1)
            act.activation(dt_e[:, :, :], dt_a[:, :, :], ACT.Exp, scale=-1.0).then_inc(act_step, 1)
            act.wait_ge(c_done, 1)
            act.activation(c_t[:, :, :].rearrange("p e n -> p (e n)"),
                           v_ps[:, :, :].rearrange("p t n -> p (t n)"), ACT.Tanh).then_inc(c_ready, 1)
            act.wait_ge(act_step, 2)
            act.activation(dt_e[:, :, :], dt_e[:, :, :], ACT.Ln, bias=1.0).then_inc(dt_log, 1)
            act.wait_ge(dt_arg, 1)
            act.activation(decay[:, :, :], dt_x[:, :, :], ACT.Exp).then_inc(decay_ready, 1)

            root(3)
            act.wait_ge(h_ready, 1)
            act.activation(gelu[:, :, :], h_pre[:, :, :], ACT.Gelu).then_inc(gelu_ready, 1)

        @block.vector
        def _(dve):
            steps = {dve_step: 0, g_step: 0}

            def chain(ins, step=dve_step):
                steps[step] += 1
                ins.then_inc(step, 1)
                dve.wait_ge(step, steps[step])

            def split_weights(hi, lo, w):
                chain(dve.tensor_copy(hi[:, :, :], w[:, :, :]))
                return dve.tensor_tensor(lo[:, :, :], w[:, :, :], hi[:, :, :], ALU.subtract)

            def high_context(par):
                return dve.tensor_copy(c_hi[par][:, :, :], raw[par][:, :, :])

            def low_context(par):
                return dve.tensor_tensor(c_lo[par][:, :, :], raw[par][:, :, :], c_hi[par][:, :, :],
                                         ALU.subtract)

            def split_context(k):
                dve.wait_ge(raw_in[k.par], 16 * k.nth)
                if k.number is None or k.number >= 2:
                    dve.wait_ge(k_done, k.c - 1)
                    dve.wait_ge(v_done, k.c - 1)
                high_context(k.par).then_inc(split_hi, 1)
                dve.wait_ge(split_hi, k.c + 1)
                low_context(k.par).then_inc(split, 1)

            def rest_of_k(par):
                for g in range(2):
                    for j in range(GP):
                        pair = slice(32 * j, 32 * j + 32)
                        last = dve.scalar_tensor_tensor(
                            out=k_stack[par][64:96, g, j, :], in0=k_ps[par][pair, g, :],
                            scalar=bk[pair, g:g + 1], in1=k_hi[par][pair, g, :],
                            op0=ALU.add, op1=ALU.subtract)
                return last

            def k_low(k):
                dve.wait_ge(k_hi_done, k.c + 1)
                wait_from(dve, scored, 4 * k.c - 4, k, 2)
                rest_of_k(k.par).then_inc(k_lo_done, 1)

            def add_bv(par):
                return dve.tensor_tensor(v_sb[par][:, :, :, 0:DH].rearrange("p t h d -> p (t h) d"),
                                         v_ps[:, :, :].rearrange("p t (h d) -> p (t h) d", d=DH),
                                         bv2[:, :, :].rearrange("p t (h d) -> p (t h) d", d=DH), ALU.add)

            def v_out(k):
                dve.wait_ge(v_done, k.c + 1)
                wait_from(dve, weighed, 4 * k.c - 4, k, 2)
                add_bv(k.par).then_inc(v_ready, 1)

            def chunk_maxima(b, to):
                return dve.tensor_reduce(to[:, 4 * b:4 * b + 4],
                                         scores[b % 2][:, :].rearrange("p (h n) -> p h n", h=4), AX_X, ALU.max)

            def layer_norm(src, nth, ps):
                chain(dve.bn_stats(stats[:, :], src[:, :]))
                chain(dve.bn_aggr(mv[:, :], stats[:, :]))
                dve.tensor_scalar(var[:, :], mv[:, 1:2], LN_EPS, None, ALU.add).then_inc(var_ready, 1)
                dve.wait_ge(std_ready, nth)
                chain(dve.reciprocal(rstd[:, :], std[:, :]))
                chain(dve.scalar_tensor_tensor(out=newton[:, :], in0=rstd[:, :], scalar=var[:, 0:1],
                                               in1=rstd[:, :], op0=ALU.mult, op1=ALU.mult))
                chain(dve.tensor_scalar(newton[:, :], newton[:, :], -0.5, 1.5, ALU.mult, ALU.add))
                chain(dve.tensor_tensor(rstd[:, :], rstd[:, :], newton[:, :], ALU.mult))
                dve.tensor_scalar(xn_tok[:, :], src[:, :], mv[:, 0:1], rstd[:, 0:1],
                                  ALU.subtract, ALU.mult).then_inc(xn_ready, 1)
                dve.wait_ge(xn_turned, nth)
                dve.tensor_copy(xn_T[:, :, :], ps[:, 0:DC * NQ].rearrange("p (k n) -> p k n", k=DC)
                                ).then_inc(xn_T_ready, 1)

            dve.wait_ge(x_in, 16)
            dve.wait_ge(wk_in, 32)
            split_weights(wk_hi, wk_lo, wk).then_inc(wk_split, 1)
            split_context(peeled(0))
            layer_norm(x_tok, 1, scores[0])
            dve.wait_ge(q_done, 1)
            dve.wait_ge(consts_in, 32)
            dve.wait_ge(wq_in, 32)
            for g in range(2):
                chain(dve.tensor_scalar(q_T[:, g, :], scores[1][:, g * NQ:(g + 1) * NQ], bq[:, g:g + 1],
                                        None, ALU.add))
            for s in range(2):
                dve.tensor_scalar(q_hi[:, :, s, :], q_T[:, :, :], side[:, s:s + 1], None,
                                  ALU.mult).then_inc(q_ready, 1)
            dve.wait_ge(q_ready, 2)
            for s in range(2):
                dve.scalar_tensor_tensor(out=q_lo[:, :, s, :], in0=q_T[:, :, :], scalar=side[:, s:s + 1],
                                         in1=q_hi[:, :, s, :], op0=ALU.mult,
                                         op1=ALU.subtract).then_inc(q_ready, 1)
            dve.wait_ge(wv_in, 48)
            split_weights(wv_hi, wv_lo, wv).then_inc(wv_split, 1)
            k_low(peeled(0))
            split_context(peeled(1))
            k_low(peeled(1))
            v_out(peeled(0))
            split_context(peeled(2))
            for b in range(4):
                dve.wait_ge(max_scored, b + 1)
                chunk_maxima(b, mx).then_inc(max_read, 1)

            def step(k):
                if k.has(1):
                    v_out(k.later(1))
                if k.has(3):
                    split_context(k.later(3))
                if k.has(2):
                    k_low(k.later(2))

            over_chunks(dve, step)

            dve.wait_ge(wo_in, 32)
            chain(dve.tensor_tensor(x_bo[:, :], x_tok[:, :], bo[:, :], ALU.add))
            heads = scores[0][:, 0:512].rearrange("p (h c) -> p h c", c=VW)

            def out_attention(turned, ready, a_turned, a_ready, done, step, between=lambda: None):
                dve.wait_ge(turned, 1)
                chain(dve.reciprocal(r_sum[:, :], heads[:, :, DH]), step)
                dve.tensor_tensor(attn[:, :].rearrange("p (h d) -> p h d", d=DH), heads[:, :, 0:DH],
                                  per_channel(r_sum, H, DH), ALU.mult).then_inc(ready, 1)
                between()
                dve.wait_ge(a_turned, 1)
                dve.tensor_copy(attn_T[:, :, :], scores[1][:, 0:DC * NQ].rearrange("p (k n) -> p k n", k=DC)
                                ).then_inc(a_ready, 1)
                dve.wait_ge(done, 1)
                chain(dve.tensor_tensor(x1[:, :], x_bo[:, :], v_ps[:, 0, :], ALU.add), step)

            def check_sums():
                chain(dve.tensor_scalar(ok[:, :], heads[:, :, DH], SUM_LIMIT, None, ALU.is_le))
                dve.tensor_reduce(ok_row[:, :], ok[:, :], AX_X, ALU.min).then_inc(ok_ready, 1)
                dve.wait_ge(ok_turned, 1)
                chain(dve.tensor_reduce(ok_all[:, :], scores[1][0:1, 512:512 + P], AX_X, ALU.min))
                dve.tensor_copy(ok_flag[:, :], ok_all[:, :]).then_inc(ok_known, 1)

            out_attention(acc_turned, attn_ready, attn_turned, attn_T_ready, wo_done, dve_step, check_sums)

            def general():
                def split_next(nth):
                    dve.wait_ge(g_raw, 16 * nth)
                    high_context(0).then_inc(g_hi, 1)
                    dve.wait_ge(g_hi, nth)
                    low_context(0).then_inc(g_split, 1)

                with dve.Fori(0, NCH) as n:
                    split_next(n + 1)
                    dve.wait_ge(g_k_hi, n + 1)
                    rest_of_k(0).then_inc(g_k_lo, 1)
                    for b in range(4):
                        dve.wait_ge(g_scored, 4 * n + (b + 1))
                        chunk_maxima(b, ok).then_inc(g_maxed, 1)
                        dve.wait_ge(g_maxed, 4 * n + (b + 1))
                        dve.tensor_tensor(mx[:, 4 * b:4 * b + 4], mx[:, 4 * b:4 * b + 4],
                                          ok[:, 4 * b:4 * b + 4], ALU.max).then_inc(g_read, 1)
                dve.wait_ge(g_shift, 1)
                dve.memset(acc[:, :, :], 0.0).then_inc(g_zeroed, 1)
                with dve.Fori(0, NCH) as n:
                    split_next(n + (NCH + 1))
                    dve.wait_ge(g_k_hi, n + (NCH + 1))
                    rest_of_k(0).then_inc(g_k_lo, 1)
                    dve.wait_ge(g_v, n + 1)
                    add_bv(0).then_inc(g_v_ready, 1)
                    dve.wait_ge(g_weighed, 4 * n + 4)
                out_attention(g_acc_turned, g_attn, g_attn_turned, g_attn_T, g_wo_done, g_step)

            unless_ok(dve, general)

            layer_norm(x1, 2, scores[1])
            dve.wait_ge(mixer_in, 16 * 12)
            chain(dve.tensor_tensor(x2[:, :], x1[:, :], out_b[:, :], ALU.add))
            dve.wait_ge(in_done_x, 1)
            dve.wait_ge(in_done_z, 1)
            dve.wait_ge(pool_const, 1)
            chain(dve.tensor_tensor(xb[:, :, TAPS - 1:], scores[0][:, 0:512].rearrange("p (e n) -> p e n", e=IC),
                                    per_channel(in_b, IC, NQ), ALU.add))
            for tap in range(TAPS):
                for e in range(IC):
                    src = xb[:, e, tap:tap + NQ]
                    w = conv_w[:, e, tap:tap + 1]
                    if tap == 0:
                        last = dve.tensor_scalar(conv[:, e, :], src, w, conv_b[:, e:e + 1], ALU.mult, ALU.add)
                    else:
                        last = dve.scalar_tensor_tensor(out=conv[:, e, :], in0=src, scalar=w,
                                                        in1=conv[:, e, :], op0=ALU.mult, op1=ALU.add)
                if tap < TAPS - 1:
                    chain(last)
            last.then_inc(conv_ready, 1)
            dve.wait_ge(z_exped, 1)
            chain(dve.tensor_scalar(z_exp[:, :, :], z_exp[:, :, :], 1.0, None, ALU.add))
            chain(dve.reciprocal(z_sig[:, :, :], z_exp[:, :, :]))
            dve.wait_ge(conv_exped, 1)
            chain(dve.tensor_scalar(c_exp[:, :, :], c_exp[:, :, :], 1.0, None, ALU.add))
            chain(dve.reciprocal(c_exp[:, :, :], c_exp[:, :, :]))
            dve.tensor_tensor(u[:, :, :], conv[:, :, :], c_exp[:, :, :], ALU.mult).then_inc(u_ready, 1)
            dve.wait_ge(u_ready, 1)
            dve.tensor_tensor(d_u[:, :, :], u[:, :, :], per_channel(d_par, IC, NQ), ALU.mult)
            dve.wait_ge(dt_done, 1)
            dve.wait_ge(b_done, 1)
            chain(dve.tensor_tensor(dt_x[:, :, :], scores[1][:, 0:512].rearrange("p (e n) -> p e n", e=IC),
                                    per_channel(dt_b, IC, NQ), ALU.add))
            dve.scalar_tensor_tensor(out=dt_a[:, :, :], in0=dt_x[:, :, :], scalar=-1.0, in1=dt_x[:, :, :],
                                     op0=ALU.mult, op1=ALU.max).then_inc(dt_abs, 1)
            dve.wait_ge(b_ready, 1)
            chain(dve.tensor_tensor(b_t[:, :, :], b_t[:, :, :], u[:, :, :], ALU.mult))
            dve.wait_ge(dt_log, 1)
            chain(dve.scalar_tensor_tensor(out=dt_x[:, :, :], in0=dt_x[:, :, :], scalar=0.0, in1=dt_e[:, :, :],
                                           op0=ALU.max, op1=ALU.add))
            dve.wait_ge(neg_a_ready, 1)
            dve.scalar_tensor_tensor(out=dt_x[:, :, :], in0=dt_x[:, :, :], scalar=1e-4,
                                     in1=per_channel(neg_a, IC, NQ), op0=ALU.add,
                                     op1=ALU.mult).then_inc(dt_arg, 1)
            dve.wait_ge(decay_ready, 1)
            chain(dve.scalar_tensor_tensor(out=b_t[:, :, :], in0=decay[:, :, :], scalar=1.0,
                                           in1=b_t[:, :, :], op0=ALU.subtract, op1=ALU.mult))
            for e in range(IC):
                last = dve.tensor_tensor_scan(states[:, e, :], decay[:, e, :], b_t[:, e, :], 0.0,
                                              ALU.mult, ALU.subtract)
            chain(last)
            dve.wait_ge(c_ready, 1)
            chain(dve.tensor_tensor(states[:, :, :], states[:, :, :], c_t[:, :, :], ALU.mult))
            chain(dve.tensor_tensor(states[:, :, :], states[:, :, :], d_u[:, :, :], ALU.add))
            chain(dve.tensor_tensor(z_sig[:, :, :], z_sig[:, :, :], states[:, :, :], ALU.mult))
            dve.tensor_copy(y_mix[:, :, :], z_sig[:, :, :]).then_inc(y_ready, 1)
            dve.wait_ge(out_proj_done, 1)
            chain(dve.tensor_tensor(x2[:, :], x2[:, :], k_ps[0][:, 0, :], ALU.add))

            layer_norm(x2, 3, scores[1])
            dve.wait_ge(ffn_in, 48)
            chain(dve.tensor_tensor(x2[:, :], x2[:, :], out_bias[:, 0, :], ALU.add))
            chain(dve.tensor_tensor(x2[:, :], x2[:, :], out_bias[:, 1, :], ALU.add))
            dve.wait_ge(h_done, 1)
            dve.tensor_tensor(h_pre[:, :, :], scores[0][:, :].rearrange("p (m n) -> p m n", m=HC),
                              per_channel(up_bias, HC, NQ), ALU.add).then_inc(h_ready, 1)
            dve.wait_ge(con_done, 1)
            dve.tensor_tensor(y_out[:, :], x2[:, :], k_ps[1][:, 0, :], ALU.add).then_inc(y_out_ready, 1)

        @block.gpsimd
        def _(pool):
            steps = [0]

            def chain(ins):
                steps[0] += 1
                ins.then_inc(butterfly, 1)
                pool.wait_ge(butterfly, steps[0])

            for t in k_stack + [q_stack]:
                flat = t[ONE_ROW:P].rearrange("p g j n -> p (g j n)") if t is not q_stack else \
                    t[ONE_ROW:P].rearrange("p g j s n -> p (g j s n)")
                chain(pool.memset(flat.bitcast(F32), 0.0))
            for t in k_stack:
                chain(pool.memset(t[ONE_ROW:ONE_ROW + 1].rearrange("p g j n -> p (g j n)").bitcast(F32), 1.0))
            for t in v_sb:
                chain(pool.memset(t[:, :, :, DH:DH + 1], 1.0))
                chain(pool.memset(t[:, :, :, DH + 1:VW], 0.0))
            chain(pool.memset(ones_row[:, :], 1.0))
            pool.memset(xb[:, :, 0:TAPS - 1], 0.0).then_inc(pool_const, 1)
            pool.wait_ge(pool_const, 1)

            for i in range(2):
                pool.dma_start(up_y[i][:, :], A["w_exp"][i]).then_inc(rows_in, 16)
                pool.dma_start(down_y[i][:, :], A["w_con"][i]).then_inc(rows_in, 16)
            pool.dma_start(up_yb[:, :], A["b_exp"]).then_inc(rows_in, 16)

            plan = [("up_w", s, s, [up_y[0], up_y[1], up_yb]) for s in range(STAGES)]
            plan += [("down_w", STAGES - 1 - s, s, [down_y[0], down_y[1]]) for s in range(STAGES - 1, -1, -1)]

            def load_stage(n):
                name, row, _, _ = plan[n]
                pool.dma_start(stage_w[n % 2][:, :, :].rearrange("p a n -> p (a n)"),
                               A[name][row].partition_broadcast(P)).then_inc(stage_in[n % 2], 16)

            load_stage(0)
            pool.wait_ge(rows_in, 16 * 5)
            for n, (_, _, s, slabs) in enumerate(plan):
                if n + 1 < len(plan):
                    load_stage(n + 1)
                pool.wait_ge(stage_in[n % 2], 16 * (n // 2 + 1))
                for y in slabs:
                    rows = y.shape[0]
                    for a in range(2):
                        last = pool.tensor_tensor(prod[a][0:rows, :], y[:, :], stage_w[n % 2][0:rows, a, :],
                                                  ALU.mult)
                    chain(last)
                    y_v = y[:, :].rearrange("p (b i s) -> p b i s", i=2, s=2 ** s)
                    for a in range(2):
                        p_v = prod[a][0:rows, :].rearrange("p (b i s) -> p b i s", i=2, s=2 ** s)
                        last = pool.tensor_tensor(y_v[:, :, a, :], p_v[:, :, 0, :], p_v[:, :, 1, :], ALU.add)
                    if n == len(plan) - 1 and y is slabs[-1]:
                        last.then_inc(butterflies_done, 1)
                    else:
                        chain(last)


def kernel(**inputs):
    import numpy as np
    import concourse.bacc as bacc
    from concourse.bass_utils import run_bass_kernel_spmd

    get = {k: np.asarray(v) for k, v in inputs.items()}
    at, mix, ffn = "L0_xattn_", "L0_attn_", "L0_ffn_"

    def rows(w):
        return np.ascontiguousarray(w.reshape(-1, P, w.shape[1]).transpose(1, 0, 2))

    def cols(b):
        return np.ascontiguousarray(b.reshape(-1, P).T)

    def stages(w, down):
        out = []
        for s in range(STAGES):
            v = w[s].reshape(HID // 2 ** (s + 1), 2 ** s, 2, 2)
            v = v.transpose(3, 0, 2, 1) if down else v.transpose(2, 0, 3, 1)
            out.append(v.reshape(2 * HID))
        return np.stack(out[::-1] if down else out)

    ctx = get["ctx_1024"][0]
    arrays = {
        "x": get["x"],
        "ctx": np.ascontiguousarray(ctx.reshape(NCH, CK, DC, P).transpose(0, 3, 2, 1)),
        "ident": np.eye(P, dtype=np.float32),
        "side": np.stack([(np.arange(P) // DH % 2 == s) for s in range(2)], 1).astype(np.float32),
        "wq": rows(get[at + "Wq"].T), "wk": rows(get[at + "Wk"].T),
        "wv": rows(get[at + "Wv"].T), "wo": rows(get[at + "Wo"].T),
        "bq": cols(get[at + "bq"]), "bk": cols(get[at + "bk"]),
        "bv": get[at + "bv"], "bo": get[at + "bo"],
        "in_w": rows(get[mix + "in_proj_w"].T), "in_b": cols(get[mix + "in_proj_b"]),
        "conv_w": rows(get[mix + "conv_w"][:, 0, :]), "conv_b": cols(get[mix + "conv_b"]),
        "dt_w": rows(get[mix + "dt_w"].T), "dt_b": cols(get[mix + "dt_b"]),
        "b_w": rows(get[mix + "b_w"].T), "c_w": rows(get[mix + "c_w"].T),
        "a_log": cols(get[mix + "A_log"]), "d_par": cols(get[mix + "D_param"]),
        "out_w": rows(get[mix + "out_w"].T), "out_b": get[mix + "out_b"],
        "w_exp": get[ffn + "W_exp"].reshape(2, P, HID),
        "b_exp": get[ffn + "b_exp"].reshape(1, HID),
        "up_w": stages(get[ffn + "up_weights"], False),
        "down_w": stages(get[ffn + "down_weights"], True),
        "up_bias": cols(get[ffn + "up_bias"]),
        "w_con": np.ascontiguousarray(get[ffn + "W_con"].T).reshape(2, P, HID),
        "b_con": get[ffn + "b_con"], "down_bias": get[ffn + "down_bias"],
    }
    nc = bacc.Bacc("TRN2", target_bir_lowering=False, num_devices=1)
    A = {k: nc.dram_tensor(k + "_dram", a.shape, F32, kind="ExternalInput").ap() for k, a in arrays.items()}
    A["out"] = nc.dram_tensor("out_dram", (1, NQ, D), F32, kind="ExternalOutput").ap()
    perceiver_block(nc, A)
    r = run_bass_kernel_spmd(nc, [{k + "_dram": np.ascontiguousarray(a) for k, a in arrays.items()}], core_ids=[0])
    return r.results[0]["out_dram"]
```

```python
from contextlib import ExitStack

import concourse.bass as bass
from concourse import mybir

F32 = mybir.dt.float32
F32R = mybir.dt.float32r
ALU = mybir.AluOpType
ACT = mybir.ActivationFunctionType
AX_X = mybir.AxisListType.X

P = 128
D = 256
DC = D // P
NQ = 128
NK = 12544
H = 16
DH = D // H
TK = 128
CT = 2
CK = TK * CT
NCH = NK // CK
GP = 4
VW = 32
STACK = 3
K_COPIES = 2 * GP
ONE_ROW = 32 * STACK
INNER = 512
IC = INNER // P
TAPS = 4
HID = 1024
HC = HID // P
STAGES = 10
LN_EPS = 1e-5
SUM_LIMIT = 1e30
SUM_LEAST = 1e-10
LOWEST = -3e38
WARM = (12, 20, 8, 10, 2)
assert NCH * CK == NK and NCH % 2 == 1 and H * DH == D and 4 * 32 == P


def perceiver_block(nc: bass.Bass, A):
    with ExitStack() as ctx:
        def sb(name, shape, dt=F32):
            return ctx.enter_context(nc.sbuf_tensor(name, shape, dt))

        def pb(name, shape, dt=F32):
            return ctx.enter_context(nc.psum_tensor(name, shape, dt))

        def sem(name):
            return ctx.enter_context(nc.semaphore(name))

        ident = sb("ident", [P, P])
        side = sb("side", [P, 2])
        x_tok = sb("x_tok", [P, D])
        xn_tok = sb("xn_tok", [P, D])
        xn_T = sb("xn_T", [P, DC, NQ])
        stats = sb("stats", [P, 6])
        mv = sb("mv", [P, 2])
        var, std, rstd, newton = (sb(n, [P, 1]) for n in ("var", "std", "rstd", "newton"))
        wq = sb("wq", [P, DC, D])
        wk = sb("wk", [P, DC, D])
        wv = sb("wv", [P, DC, D])
        wo = sb("wo", [P, DC, D])
        wk_hi = sb("wk_hi", [P, DC, D], F32R)
        wk_lo = sb("wk_lo", [P, DC, D], F32R)
        wv_hi = sb("wv_hi", [P, DC, D], F32R)
        wv_lo = sb("wv_lo", [P, DC, D], F32R)
        bq = sb("bq", [P, 2])
        bk = sb("bk", [P, 2])
        bv2 = sb("bv2", [P, CT, D])
        bo = sb("bo", [P, D])
        q_T = sb("q_T", [P, 2, NQ])
        q_hi = sb("q_hi", [P, 2, 2, NQ], F32R)
        q_lo = sb("q_lo", [P, 2, 2, NQ], F32R)
        q_stack = sb("q_stack", [P, 2, GP, 2, NQ], F32R)
        raw = [sb(f"raw{i}", [P, DC, CK]) for i in range(2)]
        c_hi = [sb(f"c_hi{i}", [P, DC, CK], F32R) for i in range(2)]
        c_lo = [sb(f"c_lo{i}", [P, DC, CK], F32R) for i in range(2)]
        k_hi = [sb(f"k_hi{i}", [P, 2, CK], F32R) for i in range(2)]
        k_stack = [sb(f"k_stack{i}", [P, 2, GP, CK], F32R) for i in range(2)]
        v_sb = [sb(f"v_sb{i}", [P, CT, H, VW]) for i in range(2)]
        probs = [sb(f"probs{i}", [P, 8, NQ]) for i in range(4)]
        mx = sb("mx", [P, H])
        neg_max = sb("neg_max", [H, NQ], F32R)
        acc_sb = sb("acc_sb", [P, 4, NQ])
        r_sum = sb("r_sum", [P, H])
        attn = sb("attn", [P, D])
        attn_T = sb("attn_T", [P, DC, NQ])
        x_bo = sb("x_bo", [P, D])
        x1 = sb("x1", [P, D])
        ok = sb("ok", [P, H])
        ok_row = sb("ok_row", [P, 1])
        ok_all = sb("ok_all", [1, 1])
        ok_flag = sb("ok_flag", [1, 1], mybir.dt.int32)

        in_w = sb("in_w", [P, DC, 2 * INNER])
        in_b = sb("in_b", [P, 2 * IC])
        conv_w = sb("conv_w", [P, IC, TAPS])
        conv_b = sb("conv_b", [P, IC])
        dt_w = sb("dt_w", [P, IC, INNER])
        b_w = sb("b_w", [P, IC, INNER])
        c_w = sb("c_w", [P, IC, INNER])
        dt_b = sb("dt_b", [P, IC])
        a_log = sb("a_log", [P, IC])
        neg_a = sb("neg_a", [P, IC])
        d_par = sb("d_par", [P, IC])
        out_w = sb("out_w", [P, IC, D])
        out_b = sb("out_b", [P, D])
        xb = sb("xb", [P, IC, TAPS - 1 + NQ])
        u = sb("u", [P, IC, NQ])
        (z_tanh, gate, conv, c_tanh, d_u, dt_x, dt_a, dt_e) = (
            probs[i // 2][:, i % 2 * IC:(i % 2 + 1) * IC, :] for i in range(8))
        (b_t, c_t, decay, states, y_mix) = (
            sb(n, [P, IC, NQ]) for n in ("b_t", "c_t", "decay", "states", "y_mix"))
        half_in_b = sb("half_in_b", [P, IC])
        half_conv_w = sb("half_conv_w", [P, IC, TAPS])
        half_conv_b = sb("half_conv_b", [P, IC])
        x2 = sb("x2", [P, D])

        up_y = [sb(f"up_y{i}", [P, HID]) for i in range(2)]
        up_b = sb("up_b", [32, 32])
        up_b_T = sb("up_b_T", [32, 32])
        up_b_parts = sb("up_b_parts", [32, 4, HC])
        up_bp = sb("up_bp", [32, 2, 32])
        up_bw = sb("up_bw", [32, STAGES, 2, 32])
        up_b_col = sb("up_b_col", [P, HC])
        down_y = [sb(f"down_y{i}", [P, HID]) for i in range(2)]
        prod = [sb(f"prod{i}", [P, HID]) for i in range(2)]
        stage_w = [sb(f"stage_w{i}", [P, 2, HID]) for i in range(2)]
        e_con = [t[:, :, :, :].rearrange("p t h c -> p (t h c)").rearrange("p (m d) -> p m d", d=D) for t in v_sb]
        up_bias = sb("up_bias", [P, HC])
        out_bias = sb("out_bias", [P, 2, D])
        h_pre, gelu = probs[0], probs[1]
        y_out = sb("y_out", [P, D])

        acc = pb("acc", [P, 4, NQ])
        scores = [pb(f"scores{i}", [P, 2 * 512]) for i in range(2)]
        k_ps = [pb(f"k_ps{i}", [P, 2, CK]) for i in range(2)]
        v_ps = pb("v_ps", [P, CT, D])

        mixer_w_in = sem("mixer_w_in")
        x_in, consts_in, wq_in, wk_in, wv_in, wo_in, mixer_in, ffn_in = (sem(n) for n in (
            "x_in", "consts_in", "wq_in", "wk_in", "wv_in", "wo_in", "mixer_in", "ffn_in"))
        raw_in = [sem("raw_in0"), sem("raw_in1")]
        stacked = [sem("stacked0"), sem("stacked1")]
        wk_split, wv_split = sem("wk_split"), sem("wv_split")
        split_hi, split = sem("split_hi"), sem("split")
        k_done, v_done = sem("k_done"), sem("v_done")
        k_hi_done, k_lo_done = sem("k_hi_done"), sem("k_lo_done")
        v_ready = sem("v_ready")
        scored, exped, weighed = sem("scored"), sem("exped"), sem("weighed")
        pool_const = sem("pool_const")
        xn_ready, xn_turned, xn_T_ready = sem("xn_ready"), sem("xn_turned"), sem("xn_T_ready")
        var_ready, std_ready = sem("var_ready"), sem("std_ready")
        q_done, q_ready = sem("q_done"), sem("q_ready")
        q_hi_stacked, q_lo_stacked = sem("q_hi_stacked"), sem("q_lo_stacked")
        max_scored, max_read, max_turned, shift_ready, shift_in = (sem(n) for n in (
            "max_scored", "max_read", "max_turned", "shift_ready", "shift_in"))
        acc_copied, acc_turned, attn_ready, attn_turned, attn_T_ready, wo_done, x1_ready = (sem(n) for n in (
            "acc_copied", "acc_turned", "attn_ready", "attn_turned", "attn_T_ready", "wo_done", "x1_ready"))
        in_done_x, in_done_z, halved, conv_ready, conv_tanhed, z_tanhed, u_ready = (sem(n) for n in (
            "in_done_x", "in_done_z", "halved", "conv_ready", "conv_tanhed", "z_tanhed", "u_ready"))
        dt_done, b_done, c_done, dt_abs, dt_log, dt_arg, decay_ready, b_ready, c_ready, neg_a_ready = (
            sem(n) for n in ("dt_done", "b_done", "c_done", "dt_abs", "dt_log", "dt_arg", "decay_ready",
                             "b_ready", "c_ready", "neg_a_ready"))
        y_ready, out_proj_done, h_done, h_ready, gelu_ready, con_done, y_out_ready, out_written = (
            sem(n) for n in ("y_ready", "out_proj_done", "h_done", "h_ready", "gelu_ready", "con_done",
                             "y_out_ready", "out_written"))
        stage_in = [sem("stage_in0"), sem("stage_in1")]
        ok_ready, ok_turned, ok_known = sem("ok_ready"), sem("ok_turned"), sem("ok_known")
        (g_raw, g_hi, g_split, g_k, g_k_hi, g_k_copied, g_k_lo, g_scored, g_read, g_v, g_v_ready, g_exped,
         g_weighed, g_turned, g_shift, g_shift_in, g_zeroed, g_acc_copied, g_acc_turned, g_attn,
         g_attn_turned, g_attn_T, g_wo_done, g_maxed) = (sem("g_" + n) for n in (
             "raw", "hi", "split", "k", "k_hi", "k_copied", "k_lo", "scored", "read", "v", "v_ready", "exped",
             "weighed", "turned", "shift", "shift_in", "zeroed", "acc_copied", "acc_turned", "attn",
             "attn_turned", "attn_T", "wo_done", "maxed"))
        g_step = sem("g_step")
        butterfly = sem("butterfly")
        rows_in = sem("rows_in")
        b_half, b_turned, b_whole, b_placed = sem("b_half"), sem("b_turned"), sem("b_whole"), sem("b_placed")
        butterflies_done = sem("butterflies_done")
        e_turned, e_copied = sem("e_turned"), sem("e_copied")
        dve_step, act_step = sem("dve_step"), sem("act_step")

        def row_on_all(name):
            return A[name].partition_broadcast(P)

        def per_channel(tile, n, width):
            return tile[:, 0:n].unsqueeze(2).broadcast_to([P, n, width])

        block = ctx.enter_context(nc.Block())
        LAST = NCH - 1

        class Chunk:

            def __init__(self, c, par, nth, number=None):
                self.c, self.par, self.nth, self.number = c, par, nth, number

            def later(self, n):
                return Chunk(self.c + n, (self.par + n) % 2, self.nth + (n + self.par) // 2,
                             None if self.number is None else self.number + n)

            def has(self, n):
                return self.number is None or self.number + n <= LAST

        def peeled(c):
            return Chunk(c, c % 2, c // 2 + 1, c)

        def over_chunks(eng, step):
            step(peeled(0))
            with eng.Fori(0, (NCH - 5) // 2) as n:
                step(Chunk(2 * n + 1, 1, n + 1))
                step(Chunk(2 * n + 2, 0, n + 2))
            for c in range(NCH - 4, NCH):
                step(peeled(c))

        def wait_from(eng, s, value, k, first):
            if k.number is None or k.number >= first:
                eng.wait_ge(s, value)

        def unless_ok(eng, general):
            eng.wait_ge(ok_known, 1)
            good = eng.value_load(ok_flag[0:1, 0:1], min_val=0, max_val=1)
            with eng.If(good == 0):
                general()
            with eng.Else():
                eng.nop()

        @block.sync
        def _(sp):
            def load_context(k):
                wait_from(sp, split, k.c - 1, k, 2)
                sp.dma_start(raw[k.par][:, :, :],
                             A["ctx"][bass.ds(k.c, 1), :, :, :].rearrange("c p k n -> (c p) k n")
                             ).then_inc(raw_in[k.par], 16)

            def copy_k_hi(par, copied):
                for r in range(2):
                    for j in range(GP):
                        sp.dma_start(k_stack[par][32 * r:32 * r + 32, :, j, :].bitcast(F32),
                                     k_hi[par][32 * j:32 * j + 32, :, :].bitcast(F32)).then_inc(copied, 16)

            def load_shift(landed):
                sp.dma_start(q_stack[ONE_ROW:ONE_ROW + 1, :, :, :, :].rearrange("o g j s q -> o (g j s q)")
                             .bitcast(F32), neg_max[:, :].bitcast(F32)).then_inc(landed, 16)

            def stack_k(k):
                sp.wait_ge(k_hi_done, k.c + 1)
                wait_from(sp, scored, 4 * k.c - 4, k, 2)
                copy_k_hi(k.par, stacked[k.par])

            sp.dma_start(x_tok[:, :], A["x"][0]).then_inc(x_in, 16)
            sp.dma_start(ident[:, :], A["ident"]).then_inc(consts_in, 16)
            sp.dma_start(wk[:, :, :], A["wk"]).then_inc(wk_in, 16)
            load_context(peeled(0))
            sp.dma_start(bk[:, :], A["bk"]).then_inc(wk_in, 16)
            sp.dma_start(side[:, :], A["side"]).then_inc(consts_in, 16)
            sp.dma_start(wq[:, :, :], A["wq"]).then_inc(wq_in, 16)
            sp.dma_start(bq[:, :], A["bq"]).then_inc(wq_in, 16)
            load_context(peeled(1))
            sp.dma_start(wv[:, :, :], A["wv"]).then_inc(wv_in, 16)
            for t in range(CT):
                sp.dma_start(bv2[:, t, :], row_on_all("bv")).then_inc(wv_in, 16)

            load_context(peeled(2))
            stack_k(peeled(0))
            sp.wait_ge(q_ready, 4)
            for j in range(GP):
                sp.dma_start(q_stack[32:64, :, j, :, :].bitcast(F32),
                             q_lo[32 * j:32 * j + 32, :, :, :].bitcast(F32)).then_inc(q_lo_stacked, 16)

            sp.wait_ge(pool_const, 1)
            sp.wait_ge(shift_ready, 1)
            load_shift(shift_in)
            load_context(peeled(3))
            stack_k(peeled(1))
            sp.dma_start(wo[:, :, :], A["wo"]).then_inc(wo_in, 16)
            sp.dma_start(bo[:, :], row_on_all("bo")).then_inc(wo_in, 16)

            def load_late():
                for to, name in ((in_w, "in_w"), (conv_w, "conv_w")):
                    sp.dma_start(to[:, :, :], A[name]).then_inc(mixer_in, 16)
                for to, name in ((in_b, "in_b"), (conv_b, "conv_b"), (dt_b, "dt_b"), (a_log, "a_log"),
                                 (d_par, "d_par")):
                    sp.dma_start(to[:, :], A[name]).then_inc(mixer_in, 16)
                for to, name in ((dt_w, "dt_w"), (b_w, "b_w"), (c_w, "c_w"), (out_w, "out_w")):
                    sp.dma_start(to[:, :, :], A[name]).then_inc(mixer_w_in, 16)
                sp.dma_start(out_b[:, :], row_on_all("out_b")).then_inc(mixer_w_in, 16)
                sp.dma_start(up_bias[:, :], A["up_bias"]).then_inc(ffn_in, 16)
                sp.dma_start(out_bias[:, 0, :], row_on_all("b_con")).then_inc(ffn_in, 16)
                sp.dma_start(out_bias[:, 1, :], row_on_all("down_bias")).then_inc(ffn_in, 16)

            def step(k):
                if k.has(4):
                    load_context(k.later(4))
                if k.has(2):
                    stack_k(k.later(2))
                if k.number == LAST - 2:
                    load_late()

            over_chunks(sp, step)

            def general():
                def load(n):
                    sp.dma_start(raw[0][:, :, :],
                                 A["ctx"][bass.ds(n, 1), :, :, :].rearrange("c p k n -> (c p) k n")
                                 ).then_inc(g_raw, 16)

                def sweep(before):
                    load(0)
                    with sp.Fori(0, NCH - 1) as n:
                        sp.wait_ge(g_k_hi, n + (before + 1))
                        copy_k_hi(0, g_k_copied)
                        load(n + 1)
                    sp.wait_ge(g_k_hi, before + NCH)
                    copy_k_hi(0, g_k_copied)

                sweep(0)
                sp.wait_ge(g_shift, 1)
                load_shift(g_shift_in)
                sweep(NCH)

            unless_ok(sp, general)
            sp.wait_ge(y_out_ready, 1)
            sp.dma_start(A["out"][0], y_out[:, :]).then_inc(out_written, 16)
            sp.wait_ge(out_written, 16)

        @block.tensor
        def _(pe):
            def times_wk(par):
                terms = ((wk_hi, c_hi), (wk_lo, c_hi), (wk_hi, c_lo))
                for g in range(2):
                    n = 0
                    for w, c in terms:
                        for kc in range(DC):
                            last = pe.matmul(k_ps[par][:, g, :], w[:, kc, g * P:(g + 1) * P],
                                             c[par][:, kc, :], start=(n == 0), stop=(n == 5))
                            n += 1
                return last

            def project_k(k):
                pe.wait_ge(split, k.c + 1)
                wait_from(pe, k_lo_done, k.c - 1, k, 2)
                times_wk(k.par).then_inc(k_done, 1)

            def times_wv(par):
                terms = ((c_hi, wv_hi), (c_hi, wv_lo), (c_lo, wv_hi))
                for t in range(CT):
                    n = 0
                    for c, w in terms:
                        for kc in range(DC):
                            last = pe.matmul(v_ps[:, t, :], c[par][:, kc, t * TK:(t + 1) * TK],
                                             w[:, kc, :], start=(n == 0), stop=(n == 5))
                            n += 1
                return last

            def project_v(k):
                pe.wait_ge(split, k.c + 1)
                wait_from(pe, v_ready, k.c, k, 1)
                times_wv(k.par).then_inc(v_done, 1)

            def times_q(par, i):
                t, g = i // 2, i % 2
                for j in range(GP):
                    last = pe.matmul(scores[i % 2][:, j * 2 * NQ:(j + 1) * 2 * NQ],
                                     k_stack[par][:, g, j, t * TK:(t + 1) * TK],
                                     q_stack[:, g, j, :, :], start=True, stop=True)
                return last

            def score(k, i):
                if i == 0:
                    pe.wait_ge(stacked[k.par], 16 * K_COPIES * k.nth)
                    pe.wait_ge(k_lo_done, k.c + 1)
                times_q(k.par, i).then_inc(scored, 1)

            def times_probs(par, i, begin=False):
                t, g = i // 2, i % 2
                for h in range(8):
                    last = pe.matmul(acc[32 * (h % 4):32 * (h % 4) + VW, 2 * g + h // 4, :],
                                     v_sb[par][:, t, 8 * g + h, :], probs[i][:, h, :],
                                     start=(begin and h < 4), stop=False, skip_group_check=True)
                return last

            def weigh(k, i, begin=False):
                times_probs(k.par, i, begin).then_inc(weighed, 1)

            def scores_by_query(b):
                for i in range(4):
                    g, j, s = b // 2, 2 * (b % 2) + i // 2, i % 2
                    last = pe.matmul(scores[b % 2][:, i * CK:(i + 1) * CK], q_stack[0:ONE_ROW, g, j, s, :],
                                     k_stack[0][0:ONE_ROW, g, j, :], start=True, stop=True)
                return last

            def out_attention(copied, turned, ready, a_turned, a_ready, done, between=lambda: None):
                pe.wait_ge(copied, 1)
                for b in range(4):
                    last = pe.transpose(scores[0][:, b * P:(b + 1) * P], acc_sb[:, b, :], ident[:, :])
                last.then_inc(turned, 1)
                pe.wait_ge(ready, 1)
                for kc in range(DC):
                    last = pe.transpose(scores[1][:, kc * NQ:(kc + 1) * NQ], attn[:, kc * P:(kc + 1) * P],
                                        ident[:, :])
                last.then_inc(a_turned, 1)
                between()
                pe.wait_ge(a_ready, 1)
                pe.wait_ge(wo_in, 32)
                for kc in range(DC):
                    last = pe.matmul(v_ps[:, 0, :], attn_T[:, kc, :], wo[:, kc, :],
                                     start=(kc == 0), stop=(kc == DC - 1))
                last.then_inc(done, 1)

            pe.wait_ge(consts_in, 32)

            def keep_warm(n):
                for _ in range(n):
                    pe.matmul(acc[:, :, :].rearrange("p a q -> p (a q)"), wk_hi[:, 0, 0:P],
                              k_stack[0][:, 0, 0:2, :].rearrange("p j n -> p (j n)"), start=True, stop=True)

            def turn_normed(nth, to):
                pe.wait_ge(xn_ready, nth)
                for kc in range(DC):
                    last = pe.transpose(to[:, kc * NQ:(kc + 1) * NQ], xn_tok[:, kc * P:(kc + 1) * P],
                                        ident[:, :])
                last.then_inc(xn_turned, 1)
                pe.wait_ge(xn_T_ready, nth)

            turn_normed(1, scores[0])
            pe.wait_ge(wk_split, 1)
            project_k(peeled(0))
            pe.wait_ge(wq_in, 32)
            for g in range(2):
                for kc in range(DC):
                    last = pe.matmul(scores[1][:, g * NQ:(g + 1) * NQ], wq[:, kc, g * P:(g + 1) * P],
                                     xn_T[:, kc, :], start=(kc == 0), stop=(kc == DC - 1))
            last.then_inc(q_done, 1)

            pe.wait_ge(k_hi_done, 1)
            pe.wait_ge(q_ready, 2)
            for j in range(GP):
                pair = slice(32 * j, 32 * j + 32)
                for g in range(2):
                    for s in range(2):
                        at = 512 * (j % 2) + (2 * g + s) * TK
                        last = pe.matmul(scores[j // 2][:, at:at + TK], q_hi[pair, g, s, :],
                                         k_hi[0][pair, g, 0:TK], start=True, stop=True)
                last.then_inc(max_scored, 1)
            pe.wait_ge(wv_split, 1)
            project_v(peeled(0))
            project_k(peeled(1))
            pe.wait_ge(max_read, GP)
            pe.transpose(acc[0:H, 0, :], mx[:, :], ident[:, :]).then_inc(max_turned, 1)

            pe.wait_ge(q_hi_stacked, 2 * GP)
            pe.wait_ge(q_lo_stacked, 16 * GP)
            pe.wait_ge(shift_in, 16)
            pe.wait_ge(pool_const, 1)

            def step(k):
                for t in range(CT):
                    for i in (2 * t, 2 * t + 1):
                        if k.number != 0 or t > 0:
                            pe.wait_ge(exped, 4 * k.c + i - 1)
                        score(k, i)
                    if t == 0 and k.number != 0:
                        for i in (2, 3):
                            weigh(k.later(1), i)
                    if t == 1:
                        pe.wait_ge(v_ready, k.c + 1)
                        for i in (0, 1):
                            weigh(k, i, begin=(k.number == 0 and i == 0))
                    if t == 0 and k.has(2):
                        project_k(k.later(2))
                    if t == 1 and k.has(1):
                        project_v(k.later(1))

            over_chunks(pe, step)
            for i in (2, 3):
                pe.wait_ge(exped, 4 * LAST + i + 1)
                weigh(peeled(LAST), i)

            def turn_ok():
                pe.wait_ge(ok_ready, 1)
                pe.transpose(scores[1][0:1, 512:512 + P], ok_row[:, :], ident[:, :]).then_inc(ok_turned, 1)

            out_attention(acc_copied, acc_turned, attn_ready, attn_turned, attn_T_ready, wo_done, turn_ok)

            def general():
                with pe.Fori(0, NCH) as n:
                    pe.wait_ge(g_split, n + 1)
                    times_wk(0).then_inc(g_k, 1)
                    pe.wait_ge(g_k_copied, 16 * K_COPIES * n + 16 * K_COPIES)
                    pe.wait_ge(g_k_lo, n + 1)
                    for b in range(4):
                        if b >= 2:
                            pe.wait_ge(g_read, 4 * n + (b - 1))
                        scores_by_query(b).then_inc(g_scored, 1)
                pe.wait_ge(g_read, 4 * NCH)
                pe.transpose(acc[0:H, 0, :], mx[:, :], ident[:, :]).then_inc(g_turned, 1)
                pe.wait_ge(g_shift_in, 16)
                pe.wait_ge(g_zeroed, 1)
                with pe.Fori(0, NCH) as n:
                    pe.wait_ge(g_split, n + (NCH + 1))
                    times_wk(0).then_inc(g_k, 1)
                    times_wv(0).then_inc(g_v, 1)
                    pe.wait_ge(g_k_copied, 16 * K_COPIES * n + 16 * K_COPIES * (NCH + 1))
                    pe.wait_ge(g_k_lo, n + (NCH + 1))
                    pe.wait_ge(g_v_ready, n + 1)
                    for i in range(4):
                        times_q(0, i).then_inc(g_scored, 1)
                        pe.wait_ge(g_exped, 4 * n + (i + 1))
                        times_probs(0, i).then_inc(g_weighed, 1)
                out_attention(g_acc_copied, g_acc_turned, g_attn, g_attn_turned, g_attn_T, g_wo_done)

            unless_ok(pe, general)

            pe.wait_ge(butterflies_done, 1)
            for b in range(4):
                if b >= 2:
                    pe.wait_ge(e_copied, b - 1)
                for i in range(4):
                    m, s = 2 * b + i // 2, i % 2
                    last = pe.transpose(k_ps[b % 2][:, i // 2, s * P:(s + 1) * P],
                                        down_y[s][:, m * P:(m + 1) * P], ident[:, :])
                last.then_inc(e_turned, 1)

            keep_warm(WARM[0])
            turn_normed(2, scores[1])
            pe.wait_ge(mixer_in, 16 * 7)
            for e in range(2 * IC):
                for kc in range(DC):
                    last = pe.matmul(scores[0][:, e * NQ:(e + 1) * NQ], in_w[:, kc, e * P:(e + 1) * P],
                                     xn_T[:, kc, :], start=(kc == 0), stop=(kc == DC - 1))
                if e == IC - 1:
                    last.then_inc(in_done_x, 1)
            last.then_inc(in_done_z, 1)

            keep_warm(WARM[1])

            pe.wait_ge(mixer_w_in, 16 * 5)
            for w, to, done in ((dt_w, scores[1][:, 0:512], dt_done), (b_w, scores[1][:, 512:1024], b_done),
                                (c_w, v_ps[:, :, :].rearrange("p t n -> p (t n)"), c_done)):
                for kc in range(IC):
                    pe.wait_ge(u_ready, kc // 2 + 1)
                    for e in range(IC):
                        last = pe.matmul(to[:, e * NQ:(e + 1) * NQ], w[:, kc, e * P:(e + 1) * P], u[:, kc, :],
                                         start=(kc == 0 and e == 0), stop=(kc == IC - 1),
                                         skip_group_check=True)
                last.then_inc(done, 1)
            keep_warm(WARM[2])
            for kc in range(IC):
                pe.wait_ge(y_ready, kc // 2 + 1)
                last = pe.matmul(k_ps[0][:, 0, :], y_mix[:, kc, :], out_w[:, kc, :],
                                 start=(kc == 0), stop=(kc == IC - 1))
            last.then_inc(out_proj_done, 1)

            keep_warm(WARM[3])
            turn_normed(3, scores[1])
            for m in range(HC):
                for kc in range(DC):
                    last = pe.matmul(scores[0][:, m * NQ:(m + 1) * NQ], up_y[kc][:, m * P:(m + 1) * P],
                                     xn_T[:, kc, :], start=(kc == 0), stop=(kc == DC - 1))
                if m % 4 == 3:
                    last.then_inc(h_done, 1)
            pe.wait_ge(e_copied, 4)
            keep_warm(WARM[4])
            for m in range(HC):
                pe.wait_ge(gelu_ready, m // 4 + 1)
                last = pe.matmul(k_ps[1][:, 0, :], gelu[:, m, :], e_con[m // 4][:, m % 4, :],
                                 start=(m == 0), stop=(m == HC - 1))
            last.then_inc(con_done, 1)

        @block.scalar
        def _(act):
            def round_k(par):
                for g in range(2):
                    last = act.activation(k_hi[par][:, g, :], k_ps[par][:, g, :], ACT.Identity,
                                          bias=bk[:, g:g + 1])
                return last

            def k_high(k):
                act.wait_ge(k_done, k.c + 1)
                wait_from(act, stacked[k.par], 16 * K_COPIES * (k.nth - 1), k, 2)
                round_k(k.par).then_inc(k_hi_done, 1)

            def exp_scores(i):
                return act.activation(probs[i][:, :, :].rearrange("p h q -> p (h q)"), scores[i % 2][:, :],
                                      ACT.Exp, scale=DH ** -0.5)

            def negate_maxima():
                return act.activation(neg_max[:, :], acc[0:H, 0, :], ACT.Copy, scale=-1.0)

            def root(nth):
                act.wait_ge(var_ready, nth)
                act.activation(std[:, :], var[:, :], ACT.Sqrt).then_inc(std_ready, 1)

            root(1)
            act.wait_ge(wk_in, 32)
            k_high(peeled(0))
            act.wait_ge(q_ready, 2)
            act.wait_ge(pool_const, 1)
            for r in (0, 2):
                for j in range(GP):
                    act.activation(q_stack[32 * r:32 * r + 32, :, j, :, :], q_hi[32 * j:32 * j + 32, :, :, :],
                                   ACT.Copy).then_inc(q_hi_stacked, 1)
            act.wait_ge(max_turned, 1)
            negate_maxima().then_inc(shift_ready, 1)
            k_high(peeled(1))

            def step(k):
                for i in range(4):
                    act.wait_ge(scored, 4 * k.c + i + 1)
                    if k.number != 0:
                        act.wait_ge(weighed, 4 * k.c + i - 3)
                    exp_scores(i).then_inc(exped, 1)
                    if i == 1 and k.has(2):
                        k_high(k.later(2))

            over_chunks(act, step)
            act.wait_ge(weighed, 4 * NCH)
            act.activation(acc_sb[:, :, :], acc[:, :, :], ACT.Copy).then_inc(acc_copied, 1)

            def general():
                with act.Fori(0, NCH) as n:
                    act.wait_ge(g_k, n + 1)
                    round_k(0).then_inc(g_k_hi, 1)
                act.wait_ge(g_turned, 1)
                negate_maxima().then_inc(g_shift, 1)
                with act.Fori(0, NCH) as n:
                    act.wait_ge(g_k, n + (NCH + 1))
                    round_k(0).then_inc(g_k_hi, 1)
                    for i in range(4):
                        act.wait_ge(g_scored, 4 * n + (4 * NCH + i + 1))
                        exp_scores(i).then_inc(g_exped, 1)
                act.wait_ge(g_weighed, 4 * NCH)
                act.activation(acc_sb[:, :, :], acc[:, :, :], ACT.Copy).then_inc(g_acc_copied, 1)

            unless_ok(act, general)

            for b in range(4):
                act.wait_ge(e_turned, b + 1)
                act.activation(e_con[b // 2][:, 2 * (b % 2):2 * (b % 2) + 2, :], k_ps[b % 2][:, :, :],
                               ACT.Copy).then_inc(e_copied, 1)

            root(2)
            act.wait_ge(mixer_in, 16 * 7)
            act.activation(half_in_b[:, :], in_b[:, IC:2 * IC], ACT.Copy, scale=0.5).then_inc(halved, 1)
            act.activation(half_conv_w[:, :, :], conv_w[:, :, :], ACT.Copy, scale=0.5).then_inc(halved, 1)
            act.activation(half_conv_b[:, :], conv_b[:, :], ACT.Copy, scale=0.5).then_inc(halved, 1)
            act.activation(neg_a[:, :], a_log[:, :], ACT.Exp).then_inc(act_step, 1)
            act.wait_ge(act_step, 1)
            act.activation(neg_a[:, :], neg_a[:, :], ACT.Copy, scale=-1.0).then_inc(neg_a_ready, 1)
            for half in range(2):
                act.wait_ge(conv_ready, half + 1)
                act.activation(c_tanh[:, 2 * half:2 * half + 2, :], conv[:, 2 * half:2 * half + 2, :],
                               ACT.Tanh).then_inc(conv_tanhed, 1)
            act.wait_ge(in_done_z, 1)
            act.wait_ge(halved, 1)
            for e in range(IC):
                last = act.activation(z_tanh[:, e, :], scores[0][:, (IC + e) * NQ:(IC + e + 1) * NQ], ACT.Tanh,
                                      scale=0.5, bias=half_in_b[:, e:e + 1])
            last.then_inc(z_tanhed, 1)
            act.preload_act_table_set("natural_log_exp_and_others")
            act.wait_ge(dt_abs, 1)
            act.activation(dt_e[:, :, :], dt_a[:, :, :], ACT.Exp, scale=-1.0).then_inc(act_step, 1)
            act.wait_ge(act_step, 2)
            act.activation(dt_e[:, :, :], dt_e[:, :, :], ACT.Ln, bias=1.0).then_inc(dt_log, 1)
            act.wait_ge(dt_arg, 1)
            act.activation(decay[:, :, :], dt_x[:, :, :], ACT.Exp).then_inc(decay_ready, 1)
            act.wait_ge(b_done, 1)
            act.activation(b_t[:, :, :].rearrange("p e n -> p (e n)"), scores[1][:, 512:1024],
                           ACT.Tanh).then_inc(b_ready, 1)
            act.wait_ge(c_done, 1)
            act.activation(c_t[:, :, :].rearrange("p e n -> p (e n)"),
                           v_ps[:, :, :].rearrange("p t n -> p (t n)"), ACT.Tanh).then_inc(c_ready, 1)

            root(3)
            for half in range(2):
                act.wait_ge(h_ready, half + 1)
                act.activation(gelu[:, 4 * half:4 * half + 4, :], h_pre[:, 4 * half:4 * half + 4, :],
                               ACT.Gelu).then_inc(gelu_ready, 1)

        @block.vector
        def _(dve):
            steps = {dve_step: 0, g_step: 0}

            def chain(ins, step=dve_step):
                steps[step] += 1
                ins.then_inc(step, 1)
                dve.wait_ge(step, steps[step])

            def split_weights(hi, lo, w):
                chain(dve.tensor_copy(hi[:, :, :], w[:, :, :]))
                return dve.tensor_tensor(lo[:, :, :], w[:, :, :], hi[:, :, :], ALU.subtract)

            def high_context(par):
                return dve.tensor_copy(c_hi[par][:, :, :], raw[par][:, :, :])

            def low_context(par):
                return dve.tensor_tensor(c_lo[par][:, :, :], raw[par][:, :, :], c_hi[par][:, :, :],
                                         ALU.subtract)

            def split_context(k):
                dve.wait_ge(raw_in[k.par], 16 * k.nth)
                if k.number is None or k.number >= 2:
                    dve.wait_ge(k_done, k.c - 1)
                    dve.wait_ge(v_done, k.c - 1)
                high_context(k.par).then_inc(split_hi, 1)
                dve.wait_ge(split_hi, k.c + 1)
                low_context(k.par).then_inc(split, 1)

            def rest_of_k(par):
                for g in range(2):
                    for j in range(GP):
                        pair = slice(32 * j, 32 * j + 32)
                        last = dve.scalar_tensor_tensor(
                            out=k_stack[par][64:96, g, j, :], in0=k_ps[par][pair, g, :],
                            scalar=bk[pair, g:g + 1], in1=k_hi[par][pair, g, :],
                            op0=ALU.add, op1=ALU.subtract)
                return last

            def k_low(k):
                dve.wait_ge(k_hi_done, k.c + 1)
                wait_from(dve, scored, 4 * k.c - 4, k, 2)
                rest_of_k(k.par).then_inc(k_lo_done, 1)

            def add_bv(par):
                return dve.tensor_tensor(v_sb[par][:, :, :, 0:DH].rearrange("p t h d -> p (t h) d"),
                                         v_ps[:, :, :].rearrange("p t (h d) -> p (t h) d", d=DH),
                                         bv2[:, :, :].rearrange("p t (h d) -> p (t h) d", d=DH), ALU.add)

            def v_out(k):
                dve.wait_ge(v_done, k.c + 1)
                wait_from(dve, weighed, 4 * k.c - 4, k, 2)
                add_bv(k.par).then_inc(v_ready, 1)

            def chunk_maxima(b, to):
                return dve.tensor_reduce(to[:, 4 * b:4 * b + 4],
                                         scores[b % 2][:, :].rearrange("p (h n) -> p h n", h=4), AX_X, ALU.max)

            def layer_norm(src, nth, ps, between=lambda: None):
                chain(dve.bn_stats(stats[:, :], src[:, :]))
                chain(dve.bn_aggr(mv[:, :], stats[:, :]))
                dve.tensor_scalar(var[:, :], mv[:, 1:2], LN_EPS, None, ALU.add).then_inc(var_ready, 1)
                dve.wait_ge(std_ready, nth)
                chain(dve.reciprocal(rstd[:, :], std[:, :]))
                chain(dve.scalar_tensor_tensor(out=newton[:, :], in0=rstd[:, :], scalar=var[:, 0:1],
                                               in1=rstd[:, :], op0=ALU.mult, op1=ALU.mult))
                chain(dve.tensor_scalar(newton[:, :], newton[:, :], -0.5, 1.5, ALU.mult, ALU.add))
                chain(dve.tensor_tensor(rstd[:, :], rstd[:, :], newton[:, :], ALU.mult))
                dve.tensor_scalar(xn_tok[:, :], src[:, :], mv[:, 0:1], rstd[:, 0:1],
                                  ALU.subtract, ALU.mult).then_inc(xn_ready, 1)
                between()
                dve.wait_ge(xn_turned, nth)
                dve.tensor_copy(xn_T[:, :, :], ps[:, 0:DC * NQ].rearrange("p (k n) -> p k n", k=DC)
                                ).then_inc(xn_T_ready, 1)

            def first_splits():
                dve.wait_ge(wk_in, 32)
                split_weights(wk_hi, wk_lo, wk).then_inc(wk_split, 1)
                split_context(peeled(0))

            dve.wait_ge(x_in, 16)
            layer_norm(x_tok, 1, scores[0], first_splits)
            dve.wait_ge(wv_in, 48)
            split_weights(wv_hi, wv_lo, wv).then_inc(wv_split, 1)
            split_context(peeled(1))
            dve.wait_ge(q_done, 1)
            dve.wait_ge(consts_in, 32)
            dve.wait_ge(wq_in, 32)
            for g in range(2):
                chain(dve.tensor_scalar(q_T[:, g, :], scores[1][:, g * NQ:(g + 1) * NQ], bq[:, g:g + 1],
                                        None, ALU.add))
            for s in range(2):
                dve.tensor_scalar(q_hi[:, :, s, :], q_T[:, :, :], side[:, s:s + 1], None,
                                  ALU.mult).then_inc(q_ready, 1)
            dve.wait_ge(q_ready, 2)
            for s in range(2):
                dve.scalar_tensor_tensor(out=q_lo[:, :, s, :], in0=q_T[:, :, :], scalar=side[:, s:s + 1],
                                         in1=q_hi[:, :, s, :], op0=ALU.mult,
                                         op1=ALU.subtract).then_inc(q_ready, 1)
            for j in range(GP):
                dve.wait_ge(max_scored, j + 1)
                dve.tensor_reduce(mx[:, :].rearrange("p (g j s) -> p j g s", g=2, j=GP)[:, j, :, :],
                                  scores[j // 2][:, 512 * (j % 2):512 * (j % 2) + 512]
                                  .rearrange("p (g s n) -> p g s n", g=2, s=2),
                                  AX_X, ALU.max).then_inc(max_read, 1)
            k_low(peeled(0))
            v_out(peeled(0))
            split_context(peeled(2))
            k_low(peeled(1))

            def step(k):
                if k.has(2):
                    k_low(k.later(2))
                if k.has(3):
                    split_context(k.later(3))
                if k.has(1):
                    v_out(k.later(1))

            over_chunks(dve, step)
            dve.wait_ge(b_half, 1)
            dve.transpose(up_b_T[:, :], up_b[:, :]).then_inc(b_turned, 1)

            dve.wait_ge(wo_in, 32)
            chain(dve.tensor_tensor(x_bo[:, :], x_tok[:, :], bo[:, :], ALU.add))
            heads = scores[0][:, 0:512].rearrange("p (h c) -> p h c", c=VW)

            def out_attention(turned, ready, a_turned, a_ready, done, step, between=lambda: None):
                dve.wait_ge(turned, 1)
                chain(dve.reciprocal(r_sum[:, :], heads[:, :, DH]), step)
                dve.tensor_tensor(attn[:, :].rearrange("p (h d) -> p h d", d=DH), heads[:, :, 0:DH],
                                  per_channel(r_sum, H, DH), ALU.mult).then_inc(ready, 1)
                between()
                dve.wait_ge(a_turned, 1)
                dve.tensor_copy(attn_T[:, :, :], scores[1][:, 0:DC * NQ].rearrange("p (k n) -> p k n", k=DC)
                                ).then_inc(a_ready, 1)
                dve.wait_ge(done, 1)
                chain(dve.tensor_tensor(x1[:, :], x_bo[:, :], v_ps[:, 0, :], ALU.add), step)

            def check_sums():
                chain(dve.tensor_scalar(ok[:, :], heads[:, :, DH], SUM_LIMIT, None, ALU.is_le))
                chain(dve.scalar_tensor_tensor(out=ok[:, :], in0=heads[:, :, DH], scalar=SUM_LEAST,
                                               in1=ok[:, :], op0=ALU.is_ge, op1=ALU.mult))
                dve.tensor_reduce(ok_row[:, :], ok[:, :], AX_X, ALU.min).then_inc(ok_ready, 1)
                dve.wait_ge(ok_turned, 1)
                chain(dve.tensor_reduce(ok_all[:, :], scores[1][0:1, 512:512 + P], AX_X, ALU.min))
                dve.tensor_copy(ok_flag[:, :], ok_all[:, :]).then_inc(ok_known, 1)

            out_attention(acc_turned, attn_ready, attn_turned, attn_T_ready, wo_done, dve_step, check_sums)

            def general():
                def split_next(nth):
                    dve.wait_ge(g_raw, 16 * nth)
                    high_context(0).then_inc(g_hi, 1)
                    dve.wait_ge(g_hi, nth)
                    low_context(0).then_inc(g_split, 1)

                chain(dve.memset(mx[:, :], LOWEST), g_step)
                with dve.Fori(0, NCH) as n:
                    split_next(n + 1)
                    dve.wait_ge(g_k_hi, n + 1)
                    rest_of_k(0).then_inc(g_k_lo, 1)
                    for b in range(4):
                        dve.wait_ge(g_scored, 4 * n + (b + 1))
                        chunk_maxima(b, ok).then_inc(g_maxed, 1)
                        dve.wait_ge(g_maxed, 4 * n + (b + 1))
                        dve.tensor_tensor(mx[:, 4 * b:4 * b + 4], mx[:, 4 * b:4 * b + 4],
                                          ok[:, 4 * b:4 * b + 4], ALU.max).then_inc(g_read, 1)
                dve.wait_ge(g_shift, 1)
                dve.memset(acc[:, :, :], 0.0).then_inc(g_zeroed, 1)
                with dve.Fori(0, NCH) as n:
                    split_next(n + (NCH + 1))
                    dve.wait_ge(g_k_hi, n + (NCH + 1))
                    rest_of_k(0).then_inc(g_k_lo, 1)
                    dve.wait_ge(g_v, n + 1)
                    add_bv(0).then_inc(g_v_ready, 1)
                    dve.wait_ge(g_weighed, 4 * n + 4)
                out_attention(g_acc_turned, g_attn, g_attn_turned, g_attn_T, g_wo_done, g_step)

            unless_ok(dve, general)

            layer_norm(x1, 2, scores[1])
            dve.wait_ge(mixer_in, 16 * 7)
            dve.wait_ge(pool_const, 1)
            dve.wait_ge(halved, 3)
            dve.wait_ge(in_done_x, 1)
            halves = [slice(2 * half, 2 * half + 2) for half in range(2)]
            for half, es in enumerate(halves):
                chain(dve.tensor_tensor(xb[:, es, TAPS - 1:],
                                        scores[0][:, 256 * half:256 * half + 256]
                                        .rearrange("p (e n) -> p e n", e=2),
                                        in_b[:, es].unsqueeze(2).broadcast_to([P, 2, NQ]), ALU.add))
                for tap in range(TAPS):
                    for e in (2 * half, 2 * half + 1):
                        src = xb[:, e, tap:tap + NQ]
                        w = half_conv_w[:, e, tap:tap + 1]
                        if tap == 0:
                            last = dve.tensor_scalar(conv[:, e, :], src, w, half_conv_b[:, e:e + 1],
                                                     ALU.mult, ALU.add)
                        else:
                            last = dve.scalar_tensor_tensor(out=conv[:, e, :], in0=src, scalar=w,
                                                            in1=conv[:, e, :], op0=ALU.mult, op1=ALU.add)
                    if tap < TAPS - 1:
                        chain(last)
                last.then_inc(conv_ready, 1)
            for half, es in enumerate(halves):
                dve.wait_ge(conv_tanhed, half + 1)
                dve.scalar_tensor_tensor(out=u[:, es, :], in0=c_tanh[:, es, :], scalar=1.0,
                                         in1=conv[:, es, :], op0=ALU.add, op1=ALU.mult).then_inc(u_ready, 1)
            dve.wait_ge(mixer_w_in, 16 * 5)
            chain(dve.tensor_tensor(x2[:, :], x1[:, :], out_b[:, :], ALU.add))
            dve.wait_ge(z_tanhed, 1)
            chain(dve.tensor_scalar(gate[:, :, :], z_tanh[:, :, :], 0.5, 0.5, ALU.mult, ALU.add))
            dve.wait_ge(u_ready, 2)
            chain(dve.tensor_tensor(d_u[:, :, :], u[:, :, :], per_channel(d_par, IC, NQ), ALU.mult))
            dve.wait_ge(dt_done, 1)
            chain(dve.tensor_tensor(dt_x[:, :, :], scores[1][:, 0:512].rearrange("p (e n) -> p e n", e=IC),
                                    per_channel(dt_b, IC, NQ), ALU.add))
            dve.scalar_tensor_tensor(out=dt_a[:, :, :], in0=dt_x[:, :, :], scalar=-1.0, in1=dt_x[:, :, :],
                                     op0=ALU.mult, op1=ALU.max).then_inc(dt_abs, 1)
            chain(dve.tensor_tensor(d_u[:, :, :], d_u[:, :, :], gate[:, :, :], ALU.mult))
            dve.wait_ge(dt_log, 1)
            dve.wait_ge(dt_abs, 1)
            chain(dve.scalar_tensor_tensor(out=dt_x[:, :, :], in0=dt_x[:, :, :], scalar=0.0, in1=dt_e[:, :, :],
                                           op0=ALU.max, op1=ALU.add))
            dve.wait_ge(neg_a_ready, 1)
            dve.scalar_tensor_tensor(out=dt_x[:, :, :], in0=dt_x[:, :, :], scalar=1e-4,
                                     in1=per_channel(neg_a, IC, NQ), op0=ALU.add,
                                     op1=ALU.mult).then_inc(dt_arg, 1)
            dve.wait_ge(b_ready, 1)
            chain(dve.tensor_tensor(b_t[:, :, :], b_t[:, :, :], u[:, :, :], ALU.mult))
            dve.wait_ge(decay_ready, 1)
            for es in halves:
                chain(dve.scalar_tensor_tensor(out=b_t[:, es, :], in0=decay[:, es, :], scalar=1.0,
                                               in1=b_t[:, es, :], op0=ALU.subtract, op1=ALU.mult))
                for e in range(es.start, es.stop):
                    last = dve.tensor_tensor_scan(states[:, e, :], decay[:, e, :], b_t[:, e, :], 0.0,
                                                  ALU.mult, ALU.subtract)
                chain(last)
                chain(dve.tensor_tensor(states[:, es, :], states[:, es, :], gate[:, es, :], ALU.mult))
            dve.wait_ge(c_ready, 1)
            for es in halves:
                chain(dve.tensor_tensor(states[:, es, :], states[:, es, :], c_t[:, es, :], ALU.mult))
                dve.tensor_tensor(y_mix[:, es, :], states[:, es, :], d_u[:, es, :], ALU.add).then_inc(y_ready, 1)
            dve.wait_ge(out_proj_done, 1)
            chain(dve.tensor_tensor(x2[:, :], x2[:, :], k_ps[0][:, 0, :], ALU.add))

            layer_norm(x2, 3, scores[1])
            dve.wait_ge(ffn_in, 48)
            dve.wait_ge(b_placed, 64)
            chain(dve.tensor_tensor(up_bias[:, :], up_bias[:, :], up_b_col[:, :], ALU.add))
            chain(dve.tensor_tensor(x2[:, :], x2[:, :], out_bias[:, 0, :], ALU.add))
            chain(dve.tensor_tensor(x2[:, :], x2[:, :], out_bias[:, 1, :], ALU.add))
            for half in range(2):
                dve.wait_ge(h_done, half + 1)
                ms = slice(4 * half, 4 * half + 4)
                dve.tensor_tensor(h_pre[:, ms, :], scores[0][:, 512 * half:512 * half + 512]
                                  .rearrange("p (m n) -> p m n", m=4),
                                  up_bias[:, ms].unsqueeze(2).broadcast_to([P, 4, NQ]),
                                  ALU.add).then_inc(h_ready, 1)
            dve.wait_ge(con_done, 1)
            dve.tensor_tensor(y_out[:, :], x2[:, :], k_ps[1][:, 0, :], ALU.add).then_inc(y_out_ready, 1)

        @block.gpsimd
        def _(pool):
            steps = [0]

            def chain(ins):
                steps[0] += 1
                ins.then_inc(butterfly, 1)
                pool.wait_ge(butterfly, steps[0])

            for t in k_stack + [q_stack]:
                flat = t[ONE_ROW:P].rearrange("p g j n -> p (g j n)") if t is not q_stack else \
                    t[ONE_ROW:P].rearrange("p g j s n -> p (g j s n)")
                chain(pool.memset(flat.bitcast(F32), 0.0))
            for t in k_stack:
                chain(pool.memset(t[ONE_ROW:ONE_ROW + 1].rearrange("p g j n -> p (g j n)").bitcast(F32), 1.0))
            for t in v_sb:
                chain(pool.memset(t[:, :, :, DH:DH + 1], 1.0))
                chain(pool.memset(t[:, :, :, DH + 1:VW], 0.0))
            pool.memset(xb[:, :, 0:TAPS - 1], 0.0).then_inc(pool_const, 1)
            pool.wait_ge(pool_const, 1)

            for i in range(2):
                pool.dma_start(up_y[i][:, :], A["w_exp"][i]).then_inc(rows_in, 16)
                pool.dma_start(down_y[i][:, :], A["w_con"][i]).then_inc(rows_in, 16)
            pool.dma_start(up_b[:, :], A["b_exp"]).then_inc(rows_in, 16)
            pool.dma_start(up_bw[:, :, :, :], A["up_wb"]).then_inc(rows_in, 16)

            plan = [("up_w", s, s, up_y) for s in range(STAGES)]
            plan += [("down_w", STAGES - 1 - s, s, down_y) for s in range(STAGES - 1, -1, -1)]

            def bias_stages(y, stages, ended):
                for s in stages:
                    for a in range(2):
                        last = pool.tensor_tensor(up_bp[:, a, :], y[:, :], up_bw[:, s, a, :], ALU.mult)
                    chain(last)
                    split_pairs = "p (b i s) -> p b i s"
                    y_v = y[:, :].rearrange(split_pairs, i=2, s=2 ** (s % 5))
                    for a in range(2):
                        p_v = up_bp[:, a, :].rearrange(split_pairs, i=2, s=2 ** (s % 5))
                        last = pool.tensor_tensor(y_v[:, :, a, :], p_v[:, :, 0, :], p_v[:, :, 1, :], ALU.add)
                    if s == stages[-1]:
                        last.then_inc(ended, 1)
                        pool.wait_ge(ended, 1)
                    else:
                        chain(last)

            def load_stage(n):
                name, row, _, _ = plan[n]
                pool.dma_start(stage_w[n % 2][:, :, :].rearrange("p a n -> p (a n)"),
                               A[name][row].partition_broadcast(P)).then_inc(stage_in[n % 2], 16)

            load_stage(0)
            pool.wait_ge(rows_in, 16 * 6)
            bias_stages(up_b, range(5), b_half)
            for n, (_, _, s, slabs) in enumerate(plan):
                if n + 1 < len(plan):
                    load_stage(n + 1)
                pool.wait_ge(stage_in[n % 2], 16 * (n // 2 + 1))
                for y in slabs:
                    for a in range(2):
                        last = pool.tensor_tensor(prod[a][:, :], y[:, :], stage_w[n % 2][:, a, :], ALU.mult)
                    chain(last)
                    y_v = y[:, :].rearrange("p (b i s) -> p b i s", i=2, s=2 ** s)
                    for a in range(2):
                        p_v = prod[a][:, :].rearrange("p (b i s) -> p b i s", i=2, s=2 ** s)
                        last = pool.tensor_tensor(y_v[:, :, a, :], p_v[:, :, 0, :], p_v[:, :, 1, :], ALU.add)
                    if n == len(plan) - 1 and y is slabs[-1]:
                        last.then_inc(butterflies_done, 1)
                        pool.wait_ge(butterflies_done, 1)
                    else:
                        chain(last)
            pool.wait_ge(b_turned, 1)
            bias_stages(up_b_T, range(5, STAGES), b_whole)
            chain(pool.tensor_copy(up_b_parts[:, :, :], up_b_T[:, :].rearrange("b (m a) -> b a m", a=4)))
            for a in range(4):
                pool.dma_start(up_b_col[32 * a:32 * a + 32, :], up_b_parts[:, a, :]).then_inc(b_placed, 16)
            pool.wait_ge(b_placed, 64)


def kernel(**inputs):
    import numpy as np
    import concourse.bacc as bacc
    from concourse.bass_utils import run_bass_kernel_spmd

    get = {k: np.asarray(v) for k, v in inputs.items()}
    at, mix, ffn = "L0_xattn_", "L0_attn_", "L0_ffn_"

    def rows(w):
        return np.ascontiguousarray(w.reshape(-1, P, w.shape[1]).transpose(1, 0, 2))

    def cols(b):
        return np.ascontiguousarray(b.reshape(-1, P).T)

    def stages(w, down):
        out = []
        for s in range(STAGES):
            v = w[s].reshape(HID // 2 ** (s + 1), 2 ** s, 2, 2)
            v = v.transpose(3, 0, 2, 1) if down else v.transpose(2, 0, 3, 1)
            out.append(v.reshape(2 * HID))
        return np.stack(out[::-1] if down else out)

    def bias_stages(w):
        rows_of = stages(w, False).reshape(STAGES, 2, 32, 32)
        low, high = rows_of[:5].transpose(2, 0, 1, 3), rows_of[5:].transpose(3, 0, 1, 2)
        return np.ascontiguousarray(np.concatenate([low, high], 1))

    ctx = get["ctx_1024"][0]
    arrays = {
        "x": get["x"],
        "ctx": np.ascontiguousarray(ctx.reshape(NCH, CK, DC, P).transpose(0, 3, 2, 1)),
        "ident": np.eye(P, dtype=np.float32),
        "side": np.stack([(np.arange(P) // DH % 2 == s) for s in range(2)], 1).astype(np.float32),
        "wq": rows(get[at + "Wq"].T), "wk": rows(get[at + "Wk"].T),
        "wv": rows(get[at + "Wv"].T), "wo": rows(get[at + "Wo"].T),
        "bq": cols(get[at + "bq"]), "bk": cols(get[at + "bk"]),
        "bv": get[at + "bv"], "bo": get[at + "bo"],
        "in_w": rows(get[mix + "in_proj_w"].T), "in_b": cols(get[mix + "in_proj_b"]),
        "conv_w": rows(get[mix + "conv_w"][:, 0, :]), "conv_b": cols(get[mix + "conv_b"]),
        "dt_w": rows(get[mix + "dt_w"].T), "dt_b": cols(get[mix + "dt_b"]),
        "b_w": rows(get[mix + "b_w"].T), "c_w": rows(get[mix + "c_w"].T),
        "a_log": cols(get[mix + "A_log"]), "d_par": cols(get[mix + "D_param"]),
        "out_w": rows(get[mix + "out_w"].T), "out_b": get[mix + "out_b"],
        "w_exp": get[ffn + "W_exp"].reshape(2, P, HID),
        "b_exp": get[ffn + "b_exp"].reshape(32, 32), "up_wb": bias_stages(get[ffn + "up_weights"]),
        "up_w": stages(get[ffn + "up_weights"], False),
        "down_w": stages(get[ffn + "down_weights"], True),
        "up_bias": cols(get[ffn + "up_bias"]),
        "w_con": np.ascontiguousarray(get[ffn + "W_con"].T).reshape(2, P, HID),
        "b_con": get[ffn + "b_con"], "down_bias": get[ffn + "down_bias"],
    }
    nc = bacc.Bacc("TRN2", target_bir_lowering=False, num_devices=1)
    A = {k: nc.dram_tensor(k + "_dram", a.shape, F32, kind="ExternalInput").ap() for k, a in arrays.items()}
    A["out"] = nc.dram_tensor("out_dram", (1, NQ, D), F32, kind="ExternalOutput").ap()
    perceiver_block(nc, A)
    r = run_bass_kernel_spmd(nc, [{k + "_dram": np.ascontiguousarray(a) for k, a in arrays.items()}], core_ids=[0])
    return r.results[0]["out_dram"]
```

```python
from contextlib import ExitStack

import concourse.bass as bass
from concourse import mybir

F32 = mybir.dt.float32
F32R = mybir.dt.float32r
ALU = mybir.AluOpType
ACT = mybir.ActivationFunctionType
AX_X = mybir.AxisListType.X

P = 128
D = 256
DC = D // P
NQ = 128
NK = 12544
H = 16
DH = D // H
TK = 128
CT = 2
CK = TK * CT
NCH = NK // CK
GP = 4
VW = 32
STACK = 3
K_COPIES = 2 * GP
ONE_ROW = 32 * STACK
INNER = 512
IC = INNER // P
TAPS = 4
HID = 1024
HC = HID // P
STAGES = 10
LN_EPS = 1e-5
SUM_LIMIT = 1e20
SUM_LEAST = 1e-10
LOWEST = -3e38
Q_ON_POOL = 2
WARM_UP = (5, 3, 5, 8)
WARM = (6, 2, 4, 9)
assert NCH * CK == NK and NCH % 2 == 1 and H * DH == D and 4 * 32 == P


def perceiver_block(nc: bass.Bass, A):
    with ExitStack() as ctx:
        def sb(name, shape, dt=F32):
            return ctx.enter_context(nc.sbuf_tensor(name, shape, dt))

        def pb(name, shape, dt=F32):
            return ctx.enter_context(nc.psum_tensor(name, shape, dt))

        def sem(name):
            return ctx.enter_context(nc.semaphore(name))

        ident = sb("ident", [P, P])
        side = sb("side", [P, 2])
        x_tok = sb("x_tok", [P, D])
        xn_tok = sb("xn_tok", [P, D])
        xn_T = sb("xn_T", [P, DC, NQ])
        stats = sb("stats", [P, 6])
        mv = sb("mv", [P, 2])
        var, std, rstd, newton = (sb(n, [P, 1]) for n in ("var", "std", "rstd", "newton"))
        wq = sb("wq", [P, DC, D])
        wk = sb("wk", [P, DC, D])
        wv = sb("wv", [P, DC, D])
        wo = sb("wo", [P, DC, D])
        wk_hi = sb("wk_hi", [P, DC, D], F32R)
        wk_lo = sb("wk_lo", [P, DC, D], F32R)
        wv_hi = sb("wv_hi", [P, DC, D], F32R)
        wv_lo = sb("wv_lo", [P, DC, D], F32R)
        bq = sb("bq", [P, 2])
        bk = sb("bk", [P, 2])
        bv2 = sb("bv2", [P, CT, D])
        bo = sb("bo", [P, D])
        q_T = sb("q_T", [P, 2, NQ])
        q_hi = sb("q_hi", [P, 2, 2, NQ], F32R)
        q_lo = sb("q_lo", [P, 2, 2, NQ], F32R)
        q_stack = sb("q_stack", [P, 2, GP, 2, NQ], F32R)
        raw = [sb(f"raw{i}", [P, DC, CK]) for i in range(2)]
        c_hi = [sb(f"c_hi{i}", [P, DC, CK], F32R) for i in range(2)]
        c_lo = [sb(f"c_lo{i}", [P, DC, CK], F32R) for i in range(2)]
        k_hi = [sb(f"k_hi{i}", [P, 2, CK], F32R) for i in range(2)]
        k_stack = [sb(f"k_stack{i}", [P, 2, GP, CK], F32R) for i in range(2)]
        v_sb = [sb(f"v_sb{i}", [P, CT, H, VW]) for i in range(2)]
        probs = [sb(f"probs{i}", [P, 8, NQ]) for i in range(4)]
        mx = sb("mx", [P, H])
        neg_max = sb("neg_max", [H, NQ], F32R)
        acc_sb = sb("acc_sb", [P, 4, NQ])
        r_sum = sb("r_sum", [P, H])
        attn = sb("attn", [P, D])
        attn_T = sb("attn_T", [P, DC, NQ])
        x_bo = sb("x_bo", [P, D])
        x1 = sb("x1", [P, D])
        ok = sb("ok", [P, H])
        ok_row = sb("ok_row", [P, 1])
        ok_all = sb("ok_all", [1, 1])
        ok_flag = sb("ok_flag", [1, 1], mybir.dt.int32)

        in_w = sb("in_w", [P, DC, 2 * INNER])
        in_b = sb("in_b", [P, 2 * IC])
        conv_w = sb("conv_w", [P, IC, TAPS])
        conv_b = sb("conv_b", [P, IC])
        dt_w = sb("dt_w", [P, IC, INNER])
        b_w = sb("b_w", [P, IC, INNER])
        c_w = sb("c_w", [P, IC, INNER])
        dt_b = sb("dt_b", [P, IC])
        a_log = sb("a_log", [P, IC])
        neg_a = sb("neg_a", [P, IC])
        d_par = sb("d_par", [P, IC])
        out_w = sb("out_w", [P, IC, D])
        out_b = sb("out_b", [P, D])
        xb = sb("xb", [P, IC, TAPS - 1 + NQ])
        u = sb("u", [P, IC, NQ])
        (z_tanh, gate, conv, c_tanh, d_u, dt_x, dt_a, dt_e) = (
            probs[i // 2][:, i % 2 * IC:(i % 2 + 1) * IC, :] for i in range(8))
        (b_t, c_t, decay, states, y_mix) = (
            sb(n, [P, IC, NQ]) for n in ("b_t", "c_t", "decay", "states", "y_mix"))
        half_in_b = sb("half_in_b", [P, IC])
        half_conv_w = sb("half_conv_w", [P, IC, TAPS])
        half_conv_b = sb("half_conv_b", [P, IC])
        x2 = sb("x2", [P, D])

        up_y = [sb(f"up_y{i}", [P, HID]) for i in range(2)]
        up_b = sb("up_b", [32, 32])
        up_b_T = sb("up_b_T", [32, 32])
        up_b_parts = sb("up_b_parts", [32, 4, HC])
        up_bp = sb("up_bp", [32, 2, 32])
        up_bw = sb("up_bw", [32, STAGES, 2, 32])
        up_b_col = sb("up_b_col", [P, HC])
        down_y = [sb(f"down_y{i}", [P, HID]) for i in range(2)]
        prod = [sb(f"prod{i}", [P, HID]) for i in range(2)]
        stage_w = [sb(f"stage_w{i}", [P, 2, HID]) for i in range(2)]
        e_con = [t[:, :, :, :].rearrange("p t h c -> p (t h c)").rearrange("p (m d) -> p m d", d=D) for t in v_sb]
        up_bias = sb("up_bias", [P, HC])
        out_bias = sb("out_bias", [P, 2, D])
        h_pre, gelu = probs[0], probs[1]
        y_out = sb("y_out", [P, D])

        acc = pb("acc", [P, 4, NQ])
        scores = [pb(f"scores{i}", [P, 2 * 512]) for i in range(2)]
        k_ps = [pb(f"k_ps{i}", [P, 2, CK]) for i in range(2)]
        v_ps = pb("v_ps", [P, CT, D])

        mixer_w_in = sem("mixer_w_in")
        x_in, ident_in, side_in, wq_in, wk_in, wv_in, wo_in, mixer_in, ffn_in = (sem(n) for n in (
            "x_in", "ident_in", "side_in", "wq_in", "wk_in", "wv_in", "wo_in", "mixer_in", "ffn_in"))
        raw_in = [sem("raw_in0"), sem("raw_in1")]
        stacked = [sem("stacked0"), sem("stacked1")]
        wk_rounded = sem("wk_rounded")
        wk_split, wv_split = sem("wk_split"), sem("wv_split")
        split_hi, split = sem("split_hi"), sem("split")
        k_done, v_done = sem("k_done"), sem("v_done")
        k_hi_done, k_lo_done = sem("k_hi_done"), sem("k_lo_done")
        v_ready = sem("v_ready")
        scored, exped, weighed = sem("scored"), sem("exped"), sem("weighed")
        pool_const = sem("pool_const")
        xn_ready, xn_turned, xn_T_ready = sem("xn_ready"), sem("xn_turned"), sem("xn_T_ready")
        var_ready, std_ready = sem("var_ready"), sem("std_ready")
        q_done, q_ready = sem("q_done"), sem("q_ready")
        q_stacked_act, q_stacked_pool = sem("q_stacked_act"), sem("q_stacked_pool")
        max_scored, max_read, max_turned, shift_ready, shift_in = (sem(n) for n in (
            "max_scored", "max_read", "max_turned", "shift_ready", "shift_in"))
        acc_copied, acc_turned, attn_ready, attn_turned, attn_T_ready, wo_done = (sem(n) for n in (
            "acc_copied", "acc_turned", "attn_ready", "attn_turned", "attn_T_ready", "wo_done"))
        in_done_x, in_done_z, halved, conv_begun, conv_ready, conv_tanhed, z_tanhed, u_ready = (sem(n) for n in (
            "in_done_x", "in_done_z", "halved", "conv_begun", "conv_ready", "conv_tanhed", "z_tanhed", "u_ready"))
        dt_done, b_done, c_done, dt_abs, dt_log, dt_arg, decay_ready, b_ready, c_ready, neg_a_ready = (
            sem(n) for n in ("dt_done", "b_done", "c_done", "dt_abs", "dt_log", "dt_arg", "decay_ready",
                             "b_ready", "c_ready", "neg_a_ready"))
        y_ready, out_proj_done, h_done, h_ready, gelu_ready, con_done, y_out_ready, out_written = (
            sem(n) for n in ("y_ready", "out_proj_done", "h_done", "h_ready", "gelu_ready", "con_done",
                             "y_out_ready", "out_written"))
        stage_in = [sem("stage_in0"), sem("stage_in1")]
        ok_ready, ok_turned, ok_known = sem("ok_ready"), sem("ok_turned"), sem("ok_known")
        (g_raw, g_hi, g_split, g_k, g_k_hi, g_k_copied, g_k_lo, g_scored, g_read, g_v, g_v_ready, g_exped,
         g_weighed, g_turned, g_shift, g_shift_in, g_zeroed, g_acc_copied, g_acc_turned, g_attn,
         g_attn_turned, g_attn_T, g_wo_done, g_maxed) = (sem("g_" + n) for n in (
             "raw", "hi", "split", "k", "k_hi", "k_copied", "k_lo", "scored", "read", "v", "v_ready", "exped",
             "weighed", "turned", "shift", "shift_in", "zeroed", "acc_copied", "acc_turned", "attn",
             "attn_turned", "attn_T", "wo_done", "maxed"))
        g_step = sem("g_step")
        butterfly = sem("butterfly")
        up_in, rows_in, down_in = sem("up_in"), sem("rows_in"), sem("down_in")
        x_begun, gate_ready, b_u_ready, c_gated = (sem(n) for n in ("x_begun", "gate_ready", "b_u_ready", "c_gated"))
        q_T_ready = sem("q_T_ready")
        b_half, b_turned, b_whole, b_placed = sem("b_half"), sem("b_turned"), sem("b_whole"), sem("b_placed")
        butterflies_done = sem("butterflies_done")
        e_turned, e_copied = sem("e_turned"), sem("e_copied")
        dve_step, act_step = sem("dve_step"), sem("act_step")

        def row_on_all(name):
            return A[name].partition_broadcast(P)

        def per_channel(tile, n, width):
            return tile[:, 0:n].unsqueeze(2).broadcast_to([P, n, width])

        in_ps = [scores[0][:, 0:256], scores[1][:, 512:768], scores[0][:, 512:768], scores[0][:, 768:1024]]
        dt_ps = [scores[1][:, 0:256], scores[0][:, 0:256]]
        b_ps = [scores[1][:, 512:768], scores[0][:, 512:768]]
        c_ps = [v_ps[:, 0, :], k_ps[1][:, 0, :]]
        h_ps = [scores[0][:, 0:256], scores[0][:, 512:768], scores[1][:, 512:768], v_ps[:, 0, :]]

        block = ctx.enter_context(nc.Block())
        LAST = NCH - 1

        PAIRS = [(g, j) for g in range(2) for j in range(GP)]

        class Chunk:

            def __init__(self, c, par, nth, number=None):
                self.c, self.par, self.nth, self.number = c, par, nth, number

            def later(self, n):
                return Chunk(self.c + n, (self.par + n) % 2, self.nth + (n + self.par) // 2,
                             None if self.number is None else self.number + n)

            def has(self, n):
                return self.number is None or self.number + n <= LAST

        def peeled(c):
            return Chunk(c, c % 2, c // 2 + 1, c)

        def over_chunks(eng, step):
            step(peeled(0))
            with eng.Fori(0, (NCH - 5) // 2) as n:
                step(Chunk(2 * n + 1, 1, n + 1))
                step(Chunk(2 * n + 2, 0, n + 2))
            for c in range(NCH - 4, NCH):
                step(peeled(c))

        def wait_from(eng, s, value, k, first):
            if k.number is None or k.number >= first:
                eng.wait_ge(s, value)

        def load_flag(eng):
            eng.wait_ge(ok_known, 1)
            return eng.value_load(ok_flag[0:1, 0:1], min_val=0, max_val=1)

        def unless_ok(eng, general, good=None):
            if good is None:
                good = load_flag(eng)
            with eng.If(good == 0):
                general()
            with eng.Else():
                eng.nop()

        @block.sync
        def _(sp):
            def load_context(k):
                wait_from(sp, split, k.c - 1, k, 2)
                sp.dma_start(raw[k.par][:, :, :],
                             A["ctx"][bass.ds(k.c, 1), :, :, :].rearrange("c p k n -> (c p) k n")
                             ).then_inc(raw_in[k.par], 16)

            def copy_k_hi(par, copied):
                for r in range(2):
                    for j in range(GP):
                        sp.dma_start(k_stack[par][32 * r:32 * r + 32, :, j, :].bitcast(F32),
                                     k_hi[par][32 * j:32 * j + 32, :, :].bitcast(F32)).then_inc(copied, 16)

            def load_shift(landed):
                sp.dma_start(q_stack[ONE_ROW:ONE_ROW + 1, :, :, :, :].rearrange("o g j s q -> o (g j s q)")
                             .bitcast(F32), neg_max[:, :].bitcast(F32)).then_inc(landed, 16)

            def stack_k(k):
                sp.wait_ge(k_hi_done, k.c + 1)
                wait_from(sp, scored, 4 * k.c - 4, k, 2)
                copy_k_hi(k.par, stacked[k.par])

            sp.dma_start(x_tok[:, :], A["x"][0]).then_inc(x_in, 16)
            sp.dma_start(ident[:, :], A["ident"]).then_inc(ident_in, 16)
            sp.dma_start(wk[:, :, :], A["wk"]).then_inc(wk_in, 16)
            load_context(peeled(0))
            sp.dma_start(bk[:, :], A["bk"]).then_inc(wk_in, 16)
            sp.dma_start(side[:, :], A["side"]).then_inc(side_in, 16)
            sp.dma_start(wq[:, :, :], A["wq"]).then_inc(wq_in, 16)
            sp.dma_start(bq[:, :], A["bq"]).then_inc(wq_in, 16)
            load_context(peeled(1))
            sp.dma_start(wv[:, :, :], A["wv"]).then_inc(wv_in, 16)
            for t in range(CT):
                sp.dma_start(bv2[:, t, :], row_on_all("bv")).then_inc(wv_in, 16)

            load_context(peeled(2))
            for i in range(2):
                sp.dma_start(up_y[i][:, :], A["w_exp"][i]).then_inc(up_in, 16)
            stack_k(peeled(0))

            sp.wait_ge(pool_const, 1)
            sp.wait_ge(shift_ready, 1)
            load_shift(shift_in)
            load_context(peeled(3))
            stack_k(peeled(1))

            def load_late():
                sp.dma_start(wo[:, :, :], A["wo"]).then_inc(wo_in, 16)
                sp.dma_start(bo[:, :], row_on_all("bo")).then_inc(wo_in, 16)
                for to, name in ((in_w, "in_w"), (conv_w, "conv_w")):
                    sp.dma_start(to[:, :, :], A[name]).then_inc(mixer_in, 16)
                for to, name in ((in_b, "in_b"), (conv_b, "conv_b"), (dt_b, "dt_b"), (a_log, "a_log"),
                                 (d_par, "d_par")):
                    sp.dma_start(to[:, :], A[name]).then_inc(mixer_in, 16)
                for to, name in ((dt_w, "dt_w"), (b_w, "b_w"), (c_w, "c_w"), (out_w, "out_w")):
                    sp.dma_start(to[:, :, :], A[name]).then_inc(mixer_w_in, 16)
                sp.dma_start(out_b[:, :], row_on_all("out_b")).then_inc(mixer_w_in, 16)
                sp.dma_start(up_bias[:, :], A["up_bias"]).then_inc(ffn_in, 16)
                sp.dma_start(out_bias[:, 0, :], row_on_all("b_con")).then_inc(ffn_in, 16)
                sp.dma_start(out_bias[:, 1, :], row_on_all("down_bias")).then_inc(ffn_in, 16)

            def step(k):
                if k.has(4):
                    load_context(k.later(4))
                if k.has(2):
                    stack_k(k.later(2))
                if k.number == LAST - 2:
                    load_late()

            over_chunks(sp, step)

            def general():
                def load(n):
                    sp.dma_start(raw[0][:, :, :],
                                 A["ctx"][bass.ds(n, 1), :, :, :].rearrange("c p k n -> (c p) k n")
                                 ).then_inc(g_raw, 16)

                def sweep(before):
                    load(0)
                    with sp.Fori(0, NCH - 1) as n:
                        sp.wait_ge(g_k_hi, n + (before + 1))
                        copy_k_hi(0, g_k_copied)
                        load(n + 1)
                    sp.wait_ge(g_k_hi, before + NCH)
                    copy_k_hi(0, g_k_copied)

                sweep(0)
                sp.wait_ge(g_shift, 1)
                load_shift(g_shift_in)
                sweep(NCH)

            unless_ok(sp, general)
            sp.wait_ge(y_out_ready, 1)
            sp.dma_start(A["out"][0], y_out[:, :]).then_inc(out_written, 16)
            sp.wait_ge(out_written, 16)

        @block.tensor
        def _(pe):
            def times_wk(par):
                terms = ((wk_hi, c_hi), (wk_lo, c_hi), (wk_hi, c_lo))
                for g in range(2):
                    n = 0
                    for w, c in terms:
                        for kc in range(DC):
                            last = pe.matmul(k_ps[par][:, g, :], w[:, kc, g * P:(g + 1) * P],
                                             c[par][:, kc, :], start=(n == 0), stop=(n == 5))
                            n += 1
                return last

            def project_k(k):
                pe.wait_ge(split, k.c + 1)
                wait_from(pe, k_lo_done, k.c - 1, k, 2)
                times_wk(k.par).then_inc(k_done, 1)

            def times_wv(par):
                terms = ((c_hi, wv_hi), (c_hi, wv_lo), (c_lo, wv_hi))
                for t in range(CT):
                    n = 0
                    for c, w in terms:
                        for kc in range(DC):
                            last = pe.matmul(v_ps[:, t, :], c[par][:, kc, t * TK:(t + 1) * TK],
                                             w[:, kc, :], start=(n == 0), stop=(n == 5))
                            n += 1
                return last

            def project_v(k):
                pe.wait_ge(split, k.c + 1)
                wait_from(pe, v_ready, k.c, k, 1)
                times_wv(k.par).then_inc(v_done, 1)

            def times_q(par, i):
                t, g = i // 2, i % 2
                for j in range(GP):
                    last = pe.matmul(scores[i % 2][:, j * 2 * NQ:(j + 1) * 2 * NQ],
                                     k_stack[par][:, g, j, t * TK:(t + 1) * TK],
                                     q_stack[:, g, j, :, :], start=True, stop=True)
                return last

            def score(k, i):
                if i == 0:
                    pe.wait_ge(stacked[k.par], 16 * K_COPIES * k.nth)
                    pe.wait_ge(k_lo_done, k.c + 1)
                times_q(k.par, i).then_inc(scored, 1)

            def times_probs(par, i, begin=False):
                t, g = i // 2, i % 2
                for h in range(8):
                    last = pe.matmul(acc[32 * (h % 4):32 * (h % 4) + VW, 2 * g + h // 4, :],
                                     v_sb[par][:, t, 8 * g + h, :], probs[i][:, h, :],
                                     start=(begin and h < 4), stop=False, skip_group_check=True)
                return last

            def weigh(k, i, begin=False):
                times_probs(k.par, i, begin).then_inc(weighed, 1)

            def scores_by_query(b):
                for i in range(4):
                    g, j, s = b // 2, 2 * (b % 2) + i // 2, i % 2
                    last = pe.matmul(scores[b % 2][:, i * CK:(i + 1) * CK], q_stack[0:ONE_ROW, g, j, s, :],
                                     k_stack[0][0:ONE_ROW, g, j, :], start=True, stop=True)
                return last

            def keep_warm(n, to=acc[:, :, :].rearrange("p a q -> p (a q)")):
                for _ in range(n):
                    pe.matmul(to, wk_hi[:, 0, 0:P], k_stack[0][:, 0, 0:2, :].rearrange("p j n -> p (j n)"),
                              start=True, stop=True)

            def out_attention(copied, turned, ready, a_turned, a_ready, done, between=lambda: None, warm=(0, 0)):
                pe.wait_ge(copied, 1)
                for b in range(4):
                    last = pe.transpose(scores[0][:, b * P:(b + 1) * P], acc_sb[:, b, :], ident[:, :])
                last.then_inc(turned, 1)
                keep_warm(warm[0])
                pe.wait_ge(ready, 1)
                for kc in range(DC):
                    last = pe.transpose(scores[1][:, kc * NQ:(kc + 1) * NQ], attn[:, kc * P:(kc + 1) * P],
                                        ident[:, :])
                last.then_inc(a_turned, 1)
                keep_warm(warm[1])
                between()
                pe.wait_ge(a_ready, 1)
                pe.wait_ge(wo_in, 32)
                for kc in range(DC):
                    last = pe.matmul(v_ps[:, 0, :], attn_T[:, kc, :], wo[:, kc, :],
                                     start=(kc == 0), stop=(kc == DC - 1))
                last.then_inc(done, 1)

            pe.wait_ge(ident_in, 16)

            def warm_up(n):
                for _ in range(n):
                    pe.matmul(acc[:, 0, :], ident[:, :], ident[:, :], start=True, stop=True)

            def turn_normed(nth, to):
                begin_to_turn(nth, to)
                pe.wait_ge(xn_T_ready, nth)

            def begin_to_turn(nth, to):
                pe.wait_ge(xn_ready, nth)
                for kc in range(DC):
                    last = pe.transpose(to[:, kc * NQ:(kc + 1) * NQ], xn_tok[:, kc * P:(kc + 1) * P],
                                        ident[:, :])
                last.then_inc(xn_turned, 1)

            warm_up(WARM_UP[0])
            begin_to_turn(1, scores[0])
            warm_up(WARM_UP[1])
            pe.wait_ge(wk_split, 1)
            project_k(peeled(0))
            pe.wait_ge(xn_T_ready, 1)
            pe.wait_ge(wq_in, 32)
            for g in range(2):
                for kc in range(DC):
                    last = pe.matmul(scores[1][:, g * NQ:(g + 1) * NQ], wq[:, kc, g * P:(g + 1) * P],
                                     xn_T[:, kc, :], start=(kc == 0), stop=(kc == DC - 1))
            last.then_inc(q_done, 1)
            project_k(peeled(1))

            pe.wait_ge(k_hi_done, 1)
            pe.wait_ge(q_ready, 2)
            for j in range(GP):
                pair = slice(32 * j, 32 * j + 32)
                for g in range(2):
                    for s in range(2):
                        at = 512 * (j % 2) + (2 * g + s) * TK
                        last = pe.matmul(scores[j // 2][:, at:at + TK], q_hi[pair, g, s, :],
                                         k_hi[0][pair, g, 0:TK], start=True, stop=True)
                last.then_inc(max_scored, 1)
            warm_up(WARM_UP[2])
            pe.wait_ge(max_read, GP)
            pe.transpose(acc[0:H, 0, :], mx[:, :], ident[:, :]).then_inc(max_turned, 1)
            pe.wait_ge(wv_split, 1)
            project_v(peeled(0))

            pe.wait_ge(shift_ready, 1)
            warm_up(WARM_UP[3])
            pe.wait_ge(q_stacked_act, 3 * GP - Q_ON_POOL)
            pe.wait_ge(q_stacked_pool, Q_ON_POOL)
            pe.wait_ge(shift_in, 16)
            pe.wait_ge(pool_const, 1)

            def step(k):
                for t in range(CT):
                    for i in (2 * t, 2 * t + 1):
                        if k.number != 0 or t > 0:
                            pe.wait_ge(exped, 4 * k.c + i - 1)
                        score(k, i)
                    if t == 0 and k.number != 0:
                        for i in (2, 3):
                            weigh(k.later(1), i)
                    if t == 1:
                        pe.wait_ge(v_ready, k.c + 1)
                        for i in (0, 1):
                            weigh(k, i, begin=(k.number == 0 and i == 0))
                    if t == 0 and k.has(2):
                        project_k(k.later(2))
                    if t == 1 and k.has(1):
                        project_v(k.later(1))

            over_chunks(pe, step)
            for i in (2, 3):
                pe.wait_ge(exped, 4 * LAST + i + 1)
                weigh(peeled(LAST), i)

            keep_warm(4, k_ps[0][:, :, :].rearrange("p g n -> p (g n)"))

            def turn_ok():
                pe.wait_ge(ok_ready, 1)
                pe.transpose(scores[1][0:1, 512:512 + P], ok_row[:, :], ident[:, :]).then_inc(ok_turned, 1)

            out_attention(acc_copied, acc_turned, attn_ready, attn_turned, attn_T_ready, wo_done, turn_ok, (4, 1))

            def general():
                with pe.Fori(0, NCH) as n:
                    pe.wait_ge(g_split, n + 1)
                    times_wk(0).then_inc(g_k, 1)
                    pe.wait_ge(g_k_copied, 16 * K_COPIES * n + 16 * K_COPIES)
                    pe.wait_ge(g_k_lo, n + 1)
                    for b in range(4):
                        if b >= 2:
                            pe.wait_ge(g_read, 4 * n + (b - 1))
                        scores_by_query(b).then_inc(g_scored, 1)
                pe.wait_ge(g_read, 4 * NCH)
                pe.transpose(acc[0:H, 0, :], mx[:, :], ident[:, :]).then_inc(g_turned, 1)
                pe.wait_ge(g_shift_in, 16)
                pe.wait_ge(g_zeroed, 1)
                with pe.Fori(0, NCH) as n:
                    pe.wait_ge(g_split, n + (NCH + 1))
                    times_wk(0).then_inc(g_k, 1)
                    times_wv(0).then_inc(g_v, 1)
                    pe.wait_ge(g_k_copied, 16 * K_COPIES * n + 16 * K_COPIES * (NCH + 1))
                    pe.wait_ge(g_k_lo, n + (NCH + 1))
                    pe.wait_ge(g_v_ready, n + 1)
                    for i in range(4):
                        times_q(0, i).then_inc(g_scored, 1)
                        pe.wait_ge(g_exped, 4 * n + (i + 1))
                        times_probs(0, i).then_inc(g_weighed, 1)
                out_attention(g_acc_copied, g_acc_turned, g_attn, g_attn_turned, g_attn_T, g_wo_done)

            unless_ok(pe, general)

            def turn_e_con(b):
                for i in range(4):
                    m, s = 2 * b + i // 2, i % 2
                    last = pe.transpose(k_ps[b % 2][:, i // 2, s * P:(s + 1) * P],
                                        down_y[s][:, m * P:(m + 1) * P], ident[:, :])
                last.then_inc(e_turned, 1)

            pe.wait_ge(butterflies_done, 1)
            turn_e_con(0)
            turn_e_con(1)

            keep_warm(WARM[0])
            turn_normed(2, scores[1])
            pe.wait_ge(mixer_in, 16 * 7)
            for e in range(2 * IC):
                for kc in range(DC):
                    last = pe.matmul(in_ps[e // 2][:, e % 2 * NQ:(e % 2 + 1) * NQ], in_w[:, kc, e * P:(e + 1) * P],
                                     xn_T[:, kc, :], start=(kc == 0), stop=(kc == DC - 1))
                if e in (1, 3):
                    last.then_inc(in_done_x, 1)
            last.then_inc(in_done_z, 1)
            for b in (2, 3):
                pe.wait_ge(e_copied, b - 1)
                turn_e_con(b)

            keep_warm(WARM[1])

            pe.wait_ge(mixer_w_in, 16 * 5)

            def inner(w, to, kcs, half):
                for e in (2 * half, 2 * half + 1):
                    for kc in kcs:
                        last = pe.matmul(to[half][:, e % 2 * NQ:(e % 2 + 1) * NQ], w[:, kc, e * P:(e + 1) * P],
                                         u[:, kc, :], start=(kc == 0 and e % 2 == 0), stop=(kc == IC - 1),
                                         skip_group_check=True)
                return last

            pe.wait_ge(u_ready, 1)
            for half in range(2):
                inner(dt_w, dt_ps, (0, 1), half)
            pe.wait_ge(u_ready, 2)
            for half in range(2):
                inner(dt_w, dt_ps, (2, 3), half).then_inc(dt_done, 1)
            pe.wait_ge(z_tanhed, 1)
            pe.wait_ge(e_copied, 4)
            for w, to, done in ((b_w, b_ps, b_done), (c_w, c_ps, c_done)):
                for half in range(2):
                    inner(w, to, range(IC), half).then_inc(done, 1)
            keep_warm(WARM[2])
            for kc in range(IC):
                pe.wait_ge(y_ready, kc // 2 + 1)
                last = pe.matmul(k_ps[0][:, 0, :], y_mix[:, kc, :], out_w[:, kc, :],
                                 start=(kc == 0), stop=(kc == IC - 1))
            last.then_inc(out_proj_done, 1)

            keep_warm(WARM[3])
            turn_normed(3, scores[1])
            for m in range(HC):
                for kc in range(DC):
                    last = pe.matmul(h_ps[m // 2][:, m % 2 * NQ:(m % 2 + 1) * NQ], up_y[kc][:, m * P:(m + 1) * P],
                                     xn_T[:, kc, :], start=(kc == 0), stop=(kc == DC - 1))
                if m % 2 == 1:
                    last.then_inc(h_done, 1)
            for m in range(HC):
                pe.wait_ge(gelu_ready, m // 2 + 1)
                last = pe.matmul(k_ps[1][:, 0, :], gelu[:, m, :], e_con[m // 4][:, m % 4, :],
                                 start=(m == 0), stop=(m == HC - 1))
            last.then_inc(con_done, 1)

        @block.scalar
        def _(act):
            def round_k(par):
                for g in range(2):
                    last = act.activation(k_hi[par][:, g, :], k_ps[par][:, g, :], ACT.Identity,
                                          bias=bk[:, g:g + 1])
                return last

            def k_high(k):
                act.wait_ge(k_done, k.c + 1)
                wait_from(act, stacked[k.par], 16 * K_COPIES * (k.nth - 1), k, 2)
                round_k(k.par).then_inc(k_hi_done, 1)

            def exp_scores(i):
                return act.activation(probs[i][:, :, :].rearrange("p h q -> p (h q)"), scores[i % 2][:, :],
                                      ACT.Exp, scale=DH ** -0.5)

            def negate_maxima():
                return act.activation(neg_max[:, :], acc[0:H, 0, :], ACT.Copy, scale=-1.0)

            def root(nth):
                act.wait_ge(var_ready, nth)
                act.activation(std[:, :], var[:, :], ACT.Sqrt).then_inc(std_ready, 1)

            root(1)
            act.wait_ge(wk_in, 32)
            act.activation(wk_hi[:, :, :], wk[:, :, :], ACT.Copy).then_inc(wk_rounded, 1)
            for par in range(2):
                act.wait_ge(raw_in[par], 16)
                act.activation(c_hi[par][:, :, :], raw[par][:, :, :], ACT.Copy).then_inc(split_hi, 1)
            k_high(peeled(0))
            act.wait_ge(wq_in, 32)
            act.wait_ge(q_done, 1)
            for g in range(2):
                act.activation(q_T[:, g, :], scores[1][:, g * NQ:(g + 1) * NQ], ACT.Identity,
                               bias=bq[:, g:g + 1]).then_inc(q_T_ready, 1)
            act.preload_act_table_set("exp_and_others")
            def stack_q(r, part, js):
                for j in js:
                    act.activation(q_stack[32 * r:32 * r + 32, :, j, :, :], part[32 * j:32 * j + 32, :, :, :],
                                   ACT.Copy).then_inc(q_stacked_act, 1)

            act.wait_ge(q_ready, 2)
            act.wait_ge(pool_const, 1)
            stack_q(0, q_hi, range(GP))
            act.wait_ge(q_ready, 4)
            k_high(peeled(1))
            stack_q(1, q_lo, (0,))
            act.wait_ge(max_turned, 1)
            negate_maxima().then_inc(shift_ready, 1)
            stack_q(1, q_lo, (1, 2, 3))
            stack_q(2, q_hi, range(Q_ON_POOL, GP))

            def step(k):
                for i in range(4):
                    act.wait_ge(scored, 4 * k.c + i + 1)
                    if k.number != 0:
                        act.wait_ge(weighed, 4 * k.c + i - 3)
                    exp_scores(i).then_inc(exped, 1)
                    if i == 1 and k.has(2):
                        k_high(k.later(2))

            over_chunks(act, step)
            act.wait_ge(weighed, 4 * NCH)
            act.activation(acc_sb[:, :, :], acc[:, :, :], ACT.Copy).then_inc(acc_copied, 1)
            act.preload_act_table_set("sqrt_and_others")

            def general():
                with act.Fori(0, NCH) as n:
                    act.wait_ge(g_k, n + 1)
                    round_k(0).then_inc(g_k_hi, 1)
                act.wait_ge(g_turned, 1)
                negate_maxima().then_inc(g_shift, 1)
                with act.Fori(0, NCH) as n:
                    act.wait_ge(g_k, n + (NCH + 1))
                    round_k(0).then_inc(g_k_hi, 1)
                    for i in range(4):
                        act.wait_ge(g_scored, 4 * n + (4 * NCH + i + 1))
                        exp_scores(i).then_inc(g_exped, 1)
                act.wait_ge(g_weighed, 4 * NCH)
                act.activation(acc_sb[:, :, :], acc[:, :, :], ACT.Copy).then_inc(g_acc_copied, 1)
                act.preload_act_table_set("sqrt_and_others")

            unless_ok(act, general)

            def copy_e_con(b):
                act.wait_ge(e_turned, b + 1)
                act.activation(e_con[b // 2][:, 2 * (b % 2):2 * (b % 2) + 2, :], k_ps[b % 2][:, :, :],
                               ACT.Copy).then_inc(e_copied, 1)

            copy_e_con(0)
            copy_e_con(1)

            root(2)
            act.wait_ge(mixer_in, 16 * 7)
            act.activation(half_in_b[:, :], in_b[:, IC:2 * IC], ACT.Copy, scale=0.5).then_inc(halved, 1)
            act.activation(half_conv_w[:, :, :], conv_w[:, :, :], ACT.Copy, scale=0.5).then_inc(halved, 1)
            act.activation(half_conv_b[:, :], conv_b[:, :], ACT.Copy, scale=0.5).then_inc(halved, 1)
            act.activation(neg_a[:, :], a_log[:, :], ACT.Exp).then_inc(act_step, 1)
            act.wait_ge(act_step, 1)
            act.activation(neg_a[:, :], neg_a[:, :], ACT.Copy, scale=-1.0).then_inc(neg_a_ready, 1)
            act.wait_ge(in_done_x, 2)
            act.wait_ge(pool_const, 1)
            for e in (2, 3):
                act.activation(xb[:, e, TAPS - 1:], in_ps[1][:, e % 2 * NQ:(e % 2 + 1) * NQ], ACT.Identity,
                               bias=in_b[:, e:e + 1]).then_inc(x_begun, 1)
            for e in (2, 3):
                act.wait_ge(x_begun, e - 1)
                act.wait_ge(halved, 3)
                act.activation(conv[:, e, :], xb[:, e, 0:NQ], ACT.Identity, scale=half_conv_w[:, e, 0:1],
                               bias=half_conv_b[:, e:e + 1]).then_inc(conv_begun, 1)
            for half in range(2):
                act.wait_ge(conv_ready, half + 1)
                act.activation(c_tanh[:, 2 * half:2 * half + 2, :], conv[:, 2 * half:2 * half + 2, :],
                               ACT.Tanh).then_inc(conv_tanhed, 1)
            act.wait_ge(in_done_z, 1)
            act.wait_ge(halved, 1)
            for e in range(IC):
                last = act.activation(z_tanh[:, e, :], in_ps[2 + e // 2][:, e % 2 * NQ:(e % 2 + 1) * NQ], ACT.Tanh,
                                      scale=0.5, bias=half_in_b[:, e:e + 1])
            last.then_inc(z_tanhed, 1)
            copy_e_con(2)
            copy_e_con(3)
            act.preload_act_table_set("natural_log_exp_and_others")
            halves = [slice(2 * half, 2 * half + 2) for half in range(2)]
            for half, es in enumerate(halves):
                act.wait_ge(dt_abs, half + 1)
                act.activation(dt_e[:, es, :], dt_a[:, es, :], ACT.Exp, scale=-1.0).then_inc(act_step, 1)
            for half, es in enumerate(halves):
                act.wait_ge(act_step, half + 2)
                act.activation(dt_e[:, es, :], dt_e[:, es, :], ACT.Ln, bias=1.0).then_inc(dt_log, 1)
            act.preload_act_table_set("exp_and_others")
            for half, es in enumerate(halves):
                act.wait_ge(dt_arg, half + 1)
                act.activation(decay[:, es, :], dt_x[:, es, :], ACT.Exp).then_inc(decay_ready, 1)
            for to, ps, done, ready in ((b_t, b_ps, b_done, b_ready), (c_t, c_ps, c_done, c_ready)):
                for half, es in enumerate(halves):
                    act.wait_ge(done, half + 1)
                    act.activation(to[:, es, :].rearrange("p e n -> p (e n)"), ps[half],
                                   ACT.Tanh).then_inc(ready, 1)

            root(3)
            for part in range(4):
                act.wait_ge(h_ready, part + 1)
                act.activation(gelu[:, 2 * part:2 * part + 2, :], h_pre[:, 2 * part:2 * part + 2, :],
                               ACT.Gelu).then_inc(gelu_ready, 1)

        @block.vector
        def _(dve):
            steps = {dve_step: 0, g_step: 0}

            def chain(ins, step=dve_step):
                steps[step] += 1
                ins.then_inc(step, 1)
                dve.wait_ge(step, steps[step])

            def split_weights(hi, lo, w):
                chain(dve.tensor_copy(hi[:, :, :], w[:, :, :]))
                return dve.tensor_tensor(lo[:, :, :], w[:, :, :], hi[:, :, :], ALU.subtract)

            def high_context(par):
                return dve.tensor_copy(c_hi[par][:, :, :], raw[par][:, :, :])

            def low_context(par):
                return dve.tensor_tensor(c_lo[par][:, :, :], raw[par][:, :, :], c_hi[par][:, :, :],
                                         ALU.subtract)

            def split_context(k):
                dve.wait_ge(raw_in[k.par], 16 * k.nth)
                if k.number is None or k.number >= 2:
                    dve.wait_ge(k_done, k.c - 1)
                    dve.wait_ge(v_done, k.c - 1)
                high_context(k.par).then_inc(split_hi, 1)
                dve.wait_ge(split_hi, k.c + 1)
                low_context(k.par).then_inc(split, 1)

            def rest_of_k(par, head_pairs=PAIRS):
                for g, j in head_pairs:
                    pair = slice(32 * j, 32 * j + 32)
                    last = dve.scalar_tensor_tensor(
                        out=k_stack[par][64:96, g, j, :], in0=k_ps[par][pair, g, :],
                        scalar=bk[pair, g:g + 1], in1=k_hi[par][pair, g, :],
                        op0=ALU.add, op1=ALU.subtract)
                return last

            def k_low_begin(k):
                dve.wait_ge(k_hi_done, k.c + 1)
                wait_from(dve, scored, 4 * k.c - 4, k, 2)
                rest_of_k(k.par, PAIRS[:6])

            def k_low_end(k):
                rest_of_k(k.par, PAIRS[6:]).then_inc(k_lo_done, 1)

            def k_low(k):
                k_low_begin(k)
                k_low_end(k)

            def add_bv(par):
                return dve.tensor_tensor(v_sb[par][:, :, :, 0:DH].rearrange("p t h d -> p (t h) d"),
                                         v_ps[:, :, :].rearrange("p t (h d) -> p (t h) d", d=DH),
                                         bv2[:, :, :].rearrange("p t (h d) -> p (t h) d", d=DH), ALU.add)

            def v_out(k):
                dve.wait_ge(v_done, k.c + 1)
                wait_from(dve, weighed, 4 * k.c - 4, k, 2)
                add_bv(k.par).then_inc(v_ready, 1)

            def chunk_maxima(b, to):
                return dve.tensor_reduce(to[:, 4 * b:4 * b + 4],
                                         scores[b % 2][:, :].rearrange("p (h n) -> p h n", h=4), AX_X, ALU.max)

            def layer_norm(src, nth, ps, between=lambda: None):
                chain(dve.bn_stats(stats[:, :], src[:, :]))
                chain(dve.bn_aggr(mv[:, :], stats[:, :]))
                dve.tensor_scalar(var[:, :], mv[:, 1:2], LN_EPS, None, ALU.add).then_inc(var_ready, 1)
                dve.wait_ge(std_ready, nth)
                chain(dve.reciprocal(rstd[:, :], std[:, :]))
                chain(dve.scalar_tensor_tensor(out=newton[:, :], in0=rstd[:, :], scalar=var[:, 0:1],
                                               in1=rstd[:, :], op0=ALU.mult, op1=ALU.mult))
                chain(dve.tensor_scalar(newton[:, :], newton[:, :], -0.5, 1.5, ALU.mult, ALU.add))
                chain(dve.tensor_tensor(rstd[:, :], rstd[:, :], newton[:, :], ALU.mult))
                dve.tensor_scalar(xn_tok[:, :], src[:, :], mv[:, 0:1], rstd[:, 0:1],
                                  ALU.subtract, ALU.mult).then_inc(xn_ready, 1)
                between()
                dve.wait_ge(xn_turned, nth)
                dve.tensor_copy(xn_T[:, :, :], ps[:, 0:DC * NQ].rearrange("p (k n) -> p k n", k=DC)
                                ).then_inc(xn_T_ready, 1)

            def lower_context(k):
                dve.wait_ge(split_hi, k.c + 1)
                low_context(k.par).then_inc(split, 1)

            def first_splits():
                dve.wait_ge(wk_rounded, 1)
                dve.tensor_tensor(wk_lo[:, :, :], wk[:, :, :], wk_hi[:, :, :], ALU.subtract).then_inc(wk_split, 1)
                lower_context(peeled(0))

            dve.wait_ge(x_in, 16)
            layer_norm(x_tok, 1, scores[0], first_splits)
            lower_context(peeled(1))
            dve.wait_ge(wv_in, 48)
            split_weights(wv_hi, wv_lo, wv).then_inc(wv_split, 1)
            dve.wait_ge(side_in, 16)
            dve.wait_ge(q_T_ready, 2)
            for s in range(2):
                dve.tensor_scalar(q_hi[:, :, s, :], q_T[:, :, :], side[:, s:s + 1], None,
                                  ALU.mult).then_inc(q_ready, 1)
            dve.wait_ge(q_ready, 2)
            for s in range(2):
                dve.scalar_tensor_tensor(out=q_lo[:, :, s, :], in0=q_T[:, :, :], scalar=side[:, s:s + 1],
                                         in1=q_hi[:, :, s, :], op0=ALU.mult,
                                         op1=ALU.subtract).then_inc(q_ready, 1)
            for j in range(GP):
                dve.wait_ge(max_scored, j + 1)
                dve.tensor_reduce(mx[:, :].rearrange("p (g j s) -> p j g s", g=2, j=GP)[:, j, :, :],
                                  scores[j // 2][:, 512 * (j % 2):512 * (j % 2) + 512]
                                  .rearrange("p (g s n) -> p g s n", g=2, s=2),
                                  AX_X, ALU.max).then_inc(max_read, 1)
            k_low(peeled(0))
            split_context(peeled(2))
            v_out(peeled(0))
            k_low(peeled(1))

            def step(k):
                if k.has(2):
                    k_low_begin(k.later(2))
                if k.has(3):
                    split_context(k.later(3))
                if k.has(2):
                    k_low_end(k.later(2))
                if k.has(1):
                    v_out(k.later(1))

            over_chunks(dve, step)
            dve.wait_ge(b_half, 1)
            dve.transpose(up_b_T[:, :], up_b[:, :]).then_inc(b_turned, 1)

            dve.wait_ge(wo_in, 32)
            chain(dve.tensor_tensor(x_bo[:, :], x_tok[:, :], bo[:, :], ALU.add))
            heads = scores[0][:, 0:512].rearrange("p (h c) -> p h c", c=VW)

            def out_attention(turned, ready, a_turned, a_ready, done, step, *between):
                dve.wait_ge(turned, 1)
                chain(dve.reciprocal(r_sum[:, :], heads[:, :, DH]), step)
                dve.tensor_tensor(attn[:, :].rearrange("p (h d) -> p h d", d=DH), heads[:, :, 0:DH],
                                  per_channel(r_sum, H, DH), ALU.mult).then_inc(ready, 1)
                for part in between[:1]:
                    part()
                dve.wait_ge(a_turned, 1)
                dve.tensor_copy(attn_T[:, :, :], scores[1][:, 0:DC * NQ].rearrange("p (k n) -> p k n", k=DC)
                                ).then_inc(a_ready, 1)
                for part in between[1:]:
                    part()
                dve.wait_ge(done, 1)
                chain(dve.tensor_tensor(x1[:, :], x_bo[:, :], v_ps[:, 0, :], ALU.add), step)

            def check_sums():
                chain(dve.tensor_scalar(ok[:, :], heads[:, :, DH], SUM_LIMIT, None, ALU.is_le))
                chain(dve.scalar_tensor_tensor(out=ok[:, :], in0=heads[:, :, DH], scalar=SUM_LEAST,
                                               in1=ok[:, :], op0=ALU.is_ge, op1=ALU.mult))
                dve.tensor_reduce(ok_row[:, :], ok[:, :], AX_X, ALU.min).then_inc(ok_ready, 1)

            def make_flag():
                dve.wait_ge(ok_turned, 1)
                chain(dve.tensor_reduce(ok_all[:, :], scores[1][0:1, 512:512 + P], AX_X, ALU.min))
                dve.tensor_copy(ok_flag[:, :], ok_all[:, :]).then_inc(ok_known, 1)

            flag = []
            out_attention(acc_turned, attn_ready, attn_turned, attn_T_ready, wo_done, dve_step, check_sums, make_flag,
                          lambda: flag.append(load_flag(dve)))

            def general():
                def split_next(nth):
                    dve.wait_ge(g_raw, 16 * nth)
                    high_context(0).then_inc(g_hi, 1)
                    dve.wait_ge(g_hi, nth)
                    low_context(0).then_inc(g_split, 1)

                chain(dve.memset(mx[:, :], LOWEST), g_step)
                with dve.Fori(0, NCH) as n:
                    split_next(n + 1)
                    dve.wait_ge(g_k_hi, n + 1)
                    rest_of_k(0).then_inc(g_k_lo, 1)
                    for b in range(4):
                        dve.wait_ge(g_scored, 4 * n + (b + 1))
                        chunk_maxima(b, ok).then_inc(g_maxed, 1)
                        dve.wait_ge(g_maxed, 4 * n + (b + 1))
                        dve.tensor_tensor(mx[:, 4 * b:4 * b + 4], mx[:, 4 * b:4 * b + 4],
                                          ok[:, 4 * b:4 * b + 4], ALU.max).then_inc(g_read, 1)
                dve.wait_ge(g_shift, 1)
                dve.memset(acc[:, :, :], 0.0).then_inc(g_zeroed, 1)
                with dve.Fori(0, NCH) as n:
                    split_next(n + (NCH + 1))
                    dve.wait_ge(g_k_hi, n + (NCH + 1))
                    rest_of_k(0).then_inc(g_k_lo, 1)
                    dve.wait_ge(g_v, n + 1)
                    add_bv(0).then_inc(g_v_ready, 1)
                    dve.wait_ge(g_weighed, 4 * n + 4)
                out_attention(g_acc_turned, g_attn, g_attn_turned, g_attn_T, g_wo_done, g_step)

            unless_ok(dve, general, flag[0])

            layer_norm(x1, 2, scores[1])
            dve.wait_ge(mixer_in, 16 * 7)
            dve.wait_ge(pool_const, 1)
            dve.wait_ge(halved, 3)
            halves = [slice(2 * half, 2 * half + 2) for half in range(2)]
            def half_u(half):
                es = halves[half]
                dve.wait_ge(conv_tanhed, half + 1)
                dve.scalar_tensor_tensor(out=u[:, es, :], in0=c_tanh[:, es, :], scalar=1.0,
                                         in1=conv[:, es, :], op0=ALU.add, op1=ALU.mult).then_inc(u_ready, 1)

            def tap(e, t):
                return dve.scalar_tensor_tensor(out=conv[:, e, :], in0=xb[:, e, t:t + NQ],
                                                scalar=half_conv_w[:, e, t:t + 1], in1=conv[:, e, :],
                                                op0=ALU.mult, op1=ALU.add)

            dve.wait_ge(in_done_x, 1)
            chain(dve.tensor_tensor(xb[:, 0:2, TAPS - 1:], in_ps[0].rearrange("p (e n) -> p e n", e=2),
                                    in_b[:, 0:2].unsqueeze(2).broadcast_to([P, 2, NQ]), ALU.add))
            for e in (0, 1):
                last = dve.tensor_scalar(conv[:, e, :], xb[:, e, 0:NQ], half_conv_w[:, e, 0:1],
                                         half_conv_b[:, e:e + 1], ALU.mult, ALU.add)
            chain(last)
            for t in range(1, TAPS):
                for e in (0, 1):
                    last = tap(e, t)
                if t < TAPS - 1:
                    chain(last)
            last.then_inc(conv_ready, 1)
            dve.wait_ge(conv_begun, 2)
            for t in range(1, TAPS):
                for e in (2, 3):
                    last = tap(e, t)
                if t < TAPS - 1:
                    chain(last)
                if t == 1:
                    half_u(0)
            last.then_inc(conv_ready, 1)
            half_u(1)
            dve.wait_ge(mixer_w_in, 16 * 5)
            chain(dve.tensor_tensor(x2[:, :], x1[:, :], out_b[:, :], ALU.add))
            dve.wait_ge(z_tanhed, 1)
            dve.tensor_scalar(gate[:, :, :], z_tanh[:, :, :], 0.5, 0.5, ALU.mult, ALU.add).then_inc(gate_ready, 1)
            dve.wait_ge(u_ready, 2)
            chain(dve.tensor_tensor(d_u[:, :, :], u[:, :, :], per_channel(d_par, IC, NQ), ALU.mult))
            for half, es in enumerate(halves):
                dve.wait_ge(dt_done, half + 1)
                chain(dve.tensor_tensor(dt_x[:, es, :], dt_ps[half].rearrange("p (e n) -> p e n", e=2),
                                        dt_b[:, es].unsqueeze(2).broadcast_to([P, 2, NQ]), ALU.add))
                dve.scalar_tensor_tensor(out=dt_a[:, es, :], in0=dt_x[:, es, :], scalar=-1.0,
                                         in1=dt_x[:, es, :], op0=ALU.mult, op1=ALU.max).then_inc(dt_abs, 1)
            dve.wait_ge(gate_ready, 1)
            chain(dve.tensor_tensor(d_u[:, :, :], d_u[:, :, :], gate[:, :, :], ALU.mult))
            dve.wait_ge(neg_a_ready, 1)
            for half, es in enumerate(halves):
                dve.wait_ge(dt_abs, half + 1)
                dve.wait_ge(dt_log, half + 1)
                chain(dve.scalar_tensor_tensor(out=dt_x[:, es, :], in0=dt_x[:, es, :], scalar=0.0,
                                               in1=dt_e[:, es, :], op0=ALU.max, op1=ALU.add))
                dve.scalar_tensor_tensor(out=dt_x[:, es, :], in0=dt_x[:, es, :], scalar=1e-4,
                                         in1=neg_a[:, es].unsqueeze(2).broadcast_to([P, 2, NQ]),
                                         op0=ALU.add, op1=ALU.mult).then_inc(dt_arg, 1)
            for half, es in enumerate(halves):
                if half == 0:
                    dve.wait_ge(b_ready, 1)
                    chain(dve.tensor_tensor(b_t[:, es, :], b_t[:, es, :], u[:, es, :], ALU.mult))
                else:
                    dve.wait_ge(b_u_ready, 1)
                dve.wait_ge(decay_ready, half + 1)
                chain(dve.scalar_tensor_tensor(out=b_t[:, es, :], in0=decay[:, es, :], scalar=1.0,
                                               in1=b_t[:, es, :], op0=ALU.subtract, op1=ALU.mult))
                for e in range(es.start, es.stop):
                    last = dve.tensor_tensor_scan(states[:, e, :], decay[:, e, :], b_t[:, e, :], 0.0,
                                                  ALU.mult, ALU.subtract)
                if half == 1:
                    chain(last)
            for half, es in enumerate(halves):
                dve.wait_ge(c_gated, half + 1)
                chain(dve.tensor_tensor(states[:, es, :], states[:, es, :], c_t[:, es, :], ALU.mult))
                dve.tensor_tensor(y_mix[:, es, :], states[:, es, :], d_u[:, es, :], ALU.add).then_inc(y_ready, 1)
            dve.wait_ge(out_proj_done, 1)
            chain(dve.tensor_tensor(x2[:, :], x2[:, :], k_ps[0][:, 0, :], ALU.add))

            layer_norm(x2, 3, scores[1])
            dve.wait_ge(ffn_in, 48)
            dve.wait_ge(b_placed, 64)
            chain(dve.tensor_tensor(up_bias[:, :], up_bias[:, :], up_b_col[:, :], ALU.add))
            chain(dve.tensor_tensor(x2[:, :], x2[:, :], out_bias[:, 0, :], ALU.add))
            chain(dve.tensor_tensor(x2[:, :], x2[:, :], out_bias[:, 1, :], ALU.add))
            for part in range(4):
                dve.wait_ge(h_done, part + 1)
                ms = slice(2 * part, 2 * part + 2)
                dve.tensor_tensor(h_pre[:, ms, :], h_ps[part].rearrange("p (m n) -> p m n", m=2),
                                  up_bias[:, ms].unsqueeze(2).broadcast_to([P, 2, NQ]),
                                  ALU.add).then_inc(h_ready, 1)
            dve.wait_ge(con_done, 1)
            dve.tensor_tensor(y_out[:, :], x2[:, :], k_ps[1][:, 0, :], ALU.add).then_inc(y_out_ready, 1)

        @block.gpsimd
        def _(pool):
            steps = [0]

            def chain(ins):
                steps[0] += 1
                ins.then_inc(butterfly, 1)
                pool.wait_ge(butterfly, steps[0])

            for t in k_stack + [q_stack]:
                flat = t[ONE_ROW:P].rearrange("p g j n -> p (g j n)") if t is not q_stack else \
                    t[ONE_ROW:P].rearrange("p g j s n -> p (g j s n)")
                chain(pool.memset(flat.bitcast(F32), 0.0))
            for t in k_stack:
                chain(pool.memset(t[ONE_ROW:ONE_ROW + 1].rearrange("p g j n -> p (g j n)").bitcast(F32), 1.0))
            for t in v_sb:
                chain(pool.memset(t[:, :, :, DH:DH + 1], 1.0))
                chain(pool.memset(t[:, :, :, DH + 1:VW], 0.0))
            pool.memset(xb[:, :, 0:TAPS - 1], 0.0).then_inc(pool_const, 1)
            pool.wait_ge(pool_const, 1)

            pool.wait_ge(q_ready, 2)
            for j in range(Q_ON_POOL):
                pool.tensor_copy(q_stack[64:96, :, j, :, :], q_hi[32 * j:32 * j + 32, :, :, :]
                                 ).then_inc(q_stacked_pool, 1)
            pool.wait_ge(shift_in, 16)
            pool.wait_ge(stacked[1], 16 * K_COPIES)
            pool.dma_start(up_b[:, :], A["b_exp"]).then_inc(rows_in, 16)
            pool.dma_start(up_bw[:, :, :, :], A["up_wb"]).then_inc(rows_in, 16)

            plan = [("up_w", s, s, up_y) for s in range(STAGES)]
            plan += [("down_w", STAGES - 1 - s, s, down_y) for s in range(STAGES - 1, -1, -1)]

            def bias_stages(y, stages, ended):
                for s in stages:
                    for a in range(2):
                        last = pool.tensor_tensor(up_bp[:, a, :], y[:, :], up_bw[:, s, a, :], ALU.mult)
                    chain(last)
                    split_pairs = "p (b i s) -> p b i s"
                    y_v = y[:, :].rearrange(split_pairs, i=2, s=2 ** (s % 5))
                    for a in range(2):
                        p_v = up_bp[:, a, :].rearrange(split_pairs, i=2, s=2 ** (s % 5))
                        last = pool.tensor_tensor(y_v[:, :, a, :], p_v[:, :, 0, :], p_v[:, :, 1, :], ALU.add)
                    if s == stages[-1]:
                        last.then_inc(ended, 1)
                        pool.wait_ge(ended, 1)
                    else:
                        chain(last)

            def load_stage(n):
                name, row, _, _ = plan[n]
                pool.dma_start(stage_w[n % 2][:, :, :].rearrange("p a n -> p (a n)"),
                               A[name][row].partition_broadcast(P)).then_inc(stage_in[n % 2], 16)

            load_stage(0)
            pool.wait_ge(rows_in, 32)
            pool.wait_ge(up_in, 32)
            bias_stages(up_b, range(5), b_half)
            for n, (_, _, s, slabs) in enumerate(plan):
                pool.wait_ge(stage_in[n % 2], 16 * (n // 2 + 1))
                if n == STAGES:
                    pool.wait_ge(down_in, 32)
                for i, y in enumerate(slabs):
                    if i == 1 and n + 1 < len(plan):
                        load_stage(n + 1)
                    if n == 2:
                        pool.dma_start(down_y[i][:, :], A["w_con"][i]).then_inc(down_in, 16)
                    for a in range(2):
                        last = pool.tensor_tensor(prod[a][:, :], y[:, :], stage_w[n % 2][:, a, :], ALU.mult)
                    chain(last)
                    y_v = y[:, :].rearrange("p (b i s) -> p b i s", i=2, s=2 ** s)
                    for a in range(2):
                        p_v = prod[a][:, :].rearrange("p (b i s) -> p b i s", i=2, s=2 ** s)
                        last = pool.tensor_tensor(y_v[:, :, a, :], p_v[:, :, 0, :], p_v[:, :, 1, :], ALU.add)
                    if n == len(plan) - 1 and y is slabs[-1]:
                        last.then_inc(butterflies_done, 1)
                        pool.wait_ge(butterflies_done, 1)
                    else:
                        chain(last)
            pool.wait_ge(b_turned, 1)
            bias_stages(up_b_T, range(5, STAGES), b_whole)
            chain(pool.tensor_copy(up_b_parts[:, :, :], up_b_T[:, :].rearrange("b (m a) -> b a m", a=4)))
            for a in range(4):
                pool.dma_start(up_b_col[32 * a:32 * a + 32, :], up_b_parts[:, a, :]).then_inc(b_placed, 16)
            pool.wait_ge(b_placed, 64)

            second = slice(2, 4)
            pool.wait_ge(u_ready, 2)
            pool.wait_ge(b_ready, 2)
            pool.tensor_tensor(b_t[:, second, :], b_t[:, second, :], u[:, second, :], ALU.mult
                               ).then_inc(b_u_ready, 1)
            pool.wait_ge(gate_ready, 1)
            for half, es in enumerate((slice(0, 2), second)):
                pool.wait_ge(c_ready, half + 1)
                pool.tensor_tensor(c_t[:, es, :], c_t[:, es, :], gate[:, es, :], ALU.mult).then_inc(c_gated, 1)


def kernel(**inputs):
    import numpy as np
    import concourse.bacc as bacc
    from concourse.bass_utils import run_bass_kernel_spmd

    get = {k: np.asarray(v) for k, v in inputs.items()}
    at, mix, ffn = "L0_xattn_", "L0_attn_", "L0_ffn_"

    def rows(w):
        return np.ascontiguousarray(w.reshape(-1, P, w.shape[1]).transpose(1, 0, 2))

    def cols(b):
        return np.ascontiguousarray(b.reshape(-1, P).T)

    def stages(w, down):
        out = []
        for s in range(STAGES):
            v = w[s].reshape(HID // 2 ** (s + 1), 2 ** s, 2, 2)
            v = v.transpose(3, 0, 2, 1) if down else v.transpose(2, 0, 3, 1)
            out.append(v.reshape(2 * HID))
        return np.stack(out[::-1] if down else out)

    def bias_stages(w):
        rows_of = stages(w, False).reshape(STAGES, 2, 32, 32)
        low, high = rows_of[:5].transpose(2, 0, 1, 3), rows_of[5:].transpose(3, 0, 1, 2)
        return np.ascontiguousarray(np.concatenate([low, high], 1))

    ctx = get["ctx_1024"][0]
    arrays = {
        "x": get["x"],
        "ctx": np.ascontiguousarray(ctx.reshape(NCH, CK, DC, P).transpose(0, 3, 2, 1)),
        "ident": np.eye(P, dtype=np.float32),
        "side": np.stack([(np.arange(P) // DH % 2 == s) for s in range(2)], 1).astype(np.float32),
        "wq": rows(get[at + "Wq"].T), "wk": rows(get[at + "Wk"].T),
        "wv": rows(get[at + "Wv"].T), "wo": rows(get[at + "Wo"].T),
        "bq": cols(get[at + "bq"]), "bk": cols(get[at + "bk"]),
        "bv": get[at + "bv"], "bo": get[at + "bo"],
        "in_w": rows(get[mix + "in_proj_w"].T), "in_b": cols(get[mix + "in_proj_b"]),
        "conv_w": rows(get[mix + "conv_w"][:, 0, :]), "conv_b": cols(get[mix + "conv_b"]),
        "dt_w": rows(get[mix + "dt_w"].T), "dt_b": cols(get[mix + "dt_b"]),
        "b_w": rows(get[mix + "b_w"].T), "c_w": rows(get[mix + "c_w"].T),
        "a_log": cols(get[mix + "A_log"]), "d_par": cols(get[mix + "D_param"]),
        "out_w": rows(get[mix + "out_w"].T), "out_b": get[mix + "out_b"],
        "w_exp": get[ffn + "W_exp"].reshape(2, P, HID),
        "b_exp": get[ffn + "b_exp"].reshape(32, 32), "up_wb": bias_stages(get[ffn + "up_weights"]),
        "up_w": stages(get[ffn + "up_weights"], False),
        "down_w": stages(get[ffn + "down_weights"], True),
        "up_bias": cols(get[ffn + "up_bias"]),
        "w_con": np.ascontiguousarray(get[ffn + "W_con"].T).reshape(2, P, HID),
        "b_con": get[ffn + "b_con"], "down_bias": get[ffn + "down_bias"],
    }
    nc = bacc.Bacc("TRN2", target_bir_lowering=False, num_devices=1)
    A = {k: nc.dram_tensor(k + "_dram", a.shape, F32, kind="ExternalInput").ap() for k, a in arrays.items()}
    A["out"] = nc.dram_tensor("out_dram", (1, NQ, D), F32, kind="ExternalOutput").ap()
    perceiver_block(nc, A)
    r = run_bass_kernel_spmd(nc, [{k + "_dram": np.ascontiguousarray(a) for k, a in arrays.items()}], core_ids=[0])
    return r.results[0]["out_dram"]
```
